# Optimizing a Trainium2 kernel written in Bass

```python
import numpy as np
import jax
import jax.numpy as jnp

def _softmax(x, axis=-1):
    return jax.nn.softmax(x, axis=axis)

def _gelu(x):
    return jax.nn.gelu(x, approximate=True)

def _silu(x):
    return jax.nn.silu(x)

def _sigmoid(x):
    return jax.nn.sigmoid(x)

def _layernorm(x, axis=-1, eps=1e-05):
    m = jnp.mean(x, axis=axis, keepdims=True)
    v = jnp.var(x, axis=axis, keepdims=True)
    return (x - m) / jnp.sqrt(v + eps)

def _scatter_add(tgt, idx, src, axis=0):
    return tgt.at[idx].add(src)

def _segment_sum(src, seg, n):
    return jax.ops.segment_sum(src, seg, n)
kernel_name = 'mk_cond_resid_d4_seqx_r8_0c6b38'

def setup_inputs(seed: int=0):
    np.random.seed(seed)
    _w = jnp.asarray

    def _rec_inputs():
        import jax
        import jax.numpy as jnp
        _rk = jax.random.key(seed)
        x = -0.000125 + 0.9999 * jax.random.normal(jax.random.fold_in(_rk, 1), (32, 32, 256), jnp.float32)
        _lenS = 32 - jax.random.randint(jax.random.fold_in(_rk, 7), (32,), 0, max(1, 32 // 4) + 1, jnp.int32)
        _lenS2 = 32 - jax.random.randint(jax.random.fold_in(_rk, 8), (32,), 0, max(1, 32 // 4) + 1, jnp.int32)
        itok_B_0_7 = jax.random.randint(jax.random.fold_in(_rk, 11), (32,), 0, 8, jnp.int32)
        fside_8xS_0 = -0.00162727 + 0.0609077 * jax.random.normal(jax.random.fold_in(_rk, 12), (8, 32), jnp.float32)
        itok_B_1_198 = jax.random.randint(jax.random.fold_in(_rk, 13), (32,), 1, 199, jnp.int32)
        itok_Bx257_0_4111 = jax.random.randint(jax.random.fold_in(_rk, 14), (32, 257), 0, 514, jnp.int32)
        itok_B_37_3939 = jax.random.randint(jax.random.fold_in(_rk, 15), (32,), 37, 3940, jnp.int32)
        itok_B_0_6 = jax.random.randint(jax.random.fold_in(_rk, 16), (32,), 0, 7, jnp.int32)
        return (x, itok_B_0_7, fside_8xS_0, itok_B_1_198, itok_Bx257_0_4111, itok_B_37_3939, itok_B_0_6)
    x, itok_B_0_7, fside_8xS_0, itok_B_1_198, itok_Bx257_0_4111, itok_B_37_3939, itok_B_0_6 = _rec_inputs()

    def _L0_cond_setup():
        import jax, jax.numpy as jnp
        import numpy as np
        B, C, T = (64, 32, 256)
        D, N = (32, 8)
        key = jax.random.key(seed)
        k_x, k_s, k_w, k_b = jax.random.split(key, 4)
        scale = 1.0 / np.sqrt(C)
        x = jax.random.normal(k_x, (B, C, T), dtype=jnp.float32)
        subjects = jax.random.randint(k_s, (B,), 0, N, dtype=jnp.int64)
        weights = jax.random.normal(k_w, (N, C, D), dtype=jnp.float32) * scale
        bias = jax.random.normal(k_b, (N, D), dtype=jnp.float32) * scale
        return {'x': x, 'subjects': subjects, 'weights': weights, 'bias': bias}
    _L0_cond_all = _L0_cond_setup()
    _L0_cond_in = {k: v for k, v in _L0_cond_all.items() if k in ('weights',)}
    del _L0_cond_all

    def _L1_cond_setup():
        import jax, jax.numpy as jnp
        import numpy as np
        B, C, T = (128, 32, 256)
        S, D = (200, 32)
        key = jax.random.key(seed)
        k1, k2, k3 = jax.random.split(key, 3)
        x = jax.random.normal(k1, (B, C, T), dtype=jnp.float32)
        conditions = jax.random.randint(k2, (B,), 0, S, dtype=jnp.int64)
        weights = jax.random.normal(k3, (S, C, D), dtype=jnp.float32) / jnp.sqrt(jnp.float32(C))
        return {'x': x, 'conditions': conditions, 'weights': weights}
    _L1_cond_all = _L1_cond_setup()
    _L1_cond_in = {k: v for k, v in _L1_cond_all.items() if k in ('weights',)}
    del _L1_cond_all

    def _L2_cond_setup():
        import jax, jax.numpy as jnp
        import numpy as np
        H, G, HD = (8, 4, 32)
        GSZ = H // G
        BLOCK = 16
        WINDOW = 128
        SCALE = 256.0 ** (-0.5)
        EPS = 1e-06
        THETA = 10000.0
        B, T, D = (16, 4, 256)
        NBLK = 257

        def _rms(x, scale):
            var = jnp.mean(x * x, axis=-1, keepdims=True)
            return x * jax.lax.rsqrt(var + EPS) * (1.0 + scale)

        def _rope(x, pos):
            half = HD // 2
            inv = 1.0 / THETA ** (jnp.arange(half, dtype=jnp.float32) / half)
            ang = pos[:, :, None].astype(jnp.float32) * inv
            cos = jnp.cos(ang)[:, None, :, :]
            sin = jnp.sin(ang)[:, None, :, :]
            x1, x2 = (x[..., :half], x[..., half:])
            return jnp.concatenate([x1 * cos - x2 * sin, x2 * cos + x1 * sin], axis=-1)
        key = jax.random.key(seed)
        ks = jax.random.split(key, 10)
        inv_d = 1.0 / np.sqrt(D)
        return {'x': jax.random.normal(ks[0], (B, T, D), jnp.float32), 'Wq': jax.random.normal(ks[1], (H * HD, D), jnp.float32) * inv_d, 'Wk': jax.random.normal(ks[2], (G * HD, D), jnp.float32) * inv_d, 'Wv': jax.random.normal(ks[3], (G * HD, D), jnp.float32) * inv_d, 'Wo': jax.random.normal(ks[4], (D, H * HD), jnp.float32) * inv_d, 'q_norm_scale': jax.random.normal(ks[5], (HD,), jnp.float32) * 0.02, 'k_norm_scale': jax.random.normal(ks[6], (HD,), jnp.float32) * 0.02, 'k_blocks': jax.random.normal(ks[7], (B * NBLK, G, BLOCK, HD), jnp.float32), 'v_blocks': jax.random.normal(ks[8], (B * NBLK, G, BLOCK, HD), jnp.float32), 'block_tables': jnp.arange(B * NBLK, dtype=jnp.int32).reshape(B, NBLK), 'kv_lens': jax.random.randint(ks[9], (B,), 0, 512, dtype=jnp.int32)}
    _L2_cond_all = _L2_cond_setup()
    _L2_cond_in = {k: v for k, v in _L2_cond_all.items() if k in ('Wq', 'Wk', 'Wv', 'Wo', 'q_norm_scale', 'k_norm_scale', 'k_blocks', 'v_blocks')}
    del _L2_cond_all

    def _L3_cond_setup():
        import jax, jax.numpy as jnp
        import numpy as np
        B, T, D_IN, D_OUT = (16, 256, 256, 256)
        N_ADAPTERS, RANK = (8, 16)
        key = jax.random.key(seed)
        k_x, k_w, k_a, k_b, k_s, k_idx = jax.random.split(key, 6)
        x = jax.random.normal(k_x, (B, T, D_IN), dtype=jnp.float32)
        W = jax.random.normal(k_w, (D_OUT, D_IN), dtype=jnp.float32) * (1.0 / np.sqrt(D_IN))
        A = jax.random.normal(k_a, (N_ADAPTERS, RANK, D_IN), dtype=jnp.float32) * 0.02
        Bm = jax.random.normal(k_b, (N_ADAPTERS, D_OUT, RANK), dtype=jnp.float32) * 0.02
        scalings = jnp.ones((N_ADAPTERS,), dtype=jnp.float32)
        adapter_idx = jax.random.randint(k_idx, (B,), 0, N_ADAPTERS, dtype=jnp.int32)
        return {'x': x, 'W': W, 'A': A, 'Bm': Bm, 'scalings': scalings, 'adapter_idx': adapter_idx}
    _L3_cond_all = _L3_cond_setup()
    _L3_cond_in = {k: v for k, v in _L3_cond_all.items() if k in ('W', 'A', 'Bm', 'scalings')}
    del _L3_cond_all
    return {'x': x, 'itok_B_0_7': itok_B_0_7, 'fside_8xS_0': fside_8xS_0, 'itok_B_1_198': itok_B_1_198, 'itok_Bx257_0_4111': itok_Bx257_0_4111, 'itok_B_37_3939': itok_B_37_3939, 'itok_B_0_6': itok_B_0_6, 'L0_cond_weights': _L0_cond_in['weights'], 'L1_cond_weights': _L1_cond_in['weights'], 'L2_cond_Wq': _L2_cond_in['Wq'], 'L2_cond_Wk': _L2_cond_in['Wk'], 'L2_cond_Wv': _L2_cond_in['Wv'], 'L2_cond_Wo': _L2_cond_in['Wo'], 'L2_cond_q_norm_scale': _L2_cond_in['q_norm_scale'], 'L2_cond_k_norm_scale': _L2_cond_in['k_norm_scale'], 'L2_cond_k_blocks': _L2_cond_in['k_blocks'], 'L2_cond_v_blocks': _L2_cond_in['v_blocks'], 'L3_cond_W': _L3_cond_in['W'], 'L3_cond_A': _L3_cond_in['A'], 'L3_cond_Bm': _L3_cond_in['Bm'], 'L3_cond_scalings': _L3_cond_in['scalings']}

def reference(x, itok_B_0_7, fside_8xS_0, itok_B_1_198, itok_Bx257_0_4111, itok_B_37_3939, itok_B_0_6, L0_cond_weights, L1_cond_weights, L2_cond_Wq, L2_cond_Wk, L2_cond_Wv, L2_cond_Wo, L2_cond_q_norm_scale, L2_cond_k_norm_scale, L2_cond_k_blocks, L2_cond_v_blocks, L3_cond_W, L3_cond_A, L3_cond_Bm, L3_cond_scalings):
    import jax
    import jax.numpy as jnp

    def _L0_cond_ref(x, subjects, weights, bias):
        import jax, jax.numpy as jnp
        import numpy as np
        B, C, T = (64, 32, 256)
        D, N = (32, 8)
        w = weights[subjects]
        b = bias[subjects]
        out = jnp.einsum('bct,bcd->bdt', x, w)
        out = out + b[:, :, None]
        return out

    def _L1_cond_ref(x, conditions, weights):
        import jax, jax.numpy as jnp
        import numpy as np
        B, C, T = (128, 32, 256)
        S, D = (200, 32)
        w = weights[conditions]
        return jnp.einsum('bct,bcd->bdt', x, w)

    def _L2_cond_ref(x, Wq, Wk, Wv, Wo, q_norm_scale, k_norm_scale, k_blocks, v_blocks, block_tables, kv_lens):
        import jax, jax.numpy as jnp
        import numpy as np
        H, G, HD = (8, 4, 32)
        GSZ = H // G
        BLOCK = 16
        WINDOW = 128
        SCALE = 256.0 ** (-0.5)
        EPS = 1e-06
        THETA = 10000.0
        B, T, D = (16, 4, 256)
        NBLK = 257

        def _rms(x, scale):
            var = jnp.mean(x * x, axis=-1, keepdims=True)
            return x * jax.lax.rsqrt(var + EPS) * (1.0 + scale)

        def _rope(x, pos):
            half = HD // 2
            inv = 1.0 / THETA ** (jnp.arange(half, dtype=jnp.float32) / half)
            ang = pos[:, :, None].astype(jnp.float32) * inv
            cos = jnp.cos(ang)[:, None, :, :]
            sin = jnp.sin(ang)[:, None, :, :]
            x1, x2 = (x[..., :half], x[..., half:])
            return jnp.concatenate([x1 * cos - x2 * sin, x2 * cos + x1 * sin], axis=-1)
        Bx, Tx, _ = x.shape
        q = jnp.einsum('btd,od->bto', x, Wq).reshape(Bx, Tx, H, HD).transpose(0, 2, 1, 3)
        k = jnp.einsum('btd,od->bto', x, Wk).reshape(Bx, Tx, G, HD).transpose(0, 2, 1, 3)
        v = jnp.einsum('btd,od->bto', x, Wv).reshape(Bx, Tx, G, HD).transpose(0, 2, 1, 3)
        q = _rms(q, q_norm_scale)
        k = _rms(k, k_norm_scale)
        pos = kv_lens[:, None] + jnp.arange(Tx, dtype=jnp.int32)
        q = _rope(q, pos)
        k = _rope(k, pos)
        slot = pos // BLOCK
        off = pos % BLOCK
        blk = jnp.take_along_axis(block_tables, slot, axis=1)
        k_blocks = k_blocks.at[blk, :, off, :].set(k.transpose(0, 2, 1, 3))
        v_blocks = v_blocks.at[blk, :, off, :].set(v.transpose(0, 2, 1, 3))
        k_all = k_blocks[block_tables].transpose(0, 2, 1, 3, 4).reshape(Bx, G, -1, HD)
        v_all = v_blocks[block_tables].transpose(0, 2, 1, 3, 4).reshape(Bx, G, -1, HD)
        S = k_all.shape[2]
        qg = q.reshape(Bx, G, GSZ, Tx, HD)
        scores = jnp.einsum('bghtd,bgsd->bghts', qg, k_all) * SCALE
        kpos = jnp.arange(S, dtype=jnp.int32)
        allowed = (kpos[None, None, :] <= pos[:, :, None]) & (kpos[None, None, :] > pos[:, :, None] - WINDOW)
        scores = jnp.where(allowed[:, None, None, :, :], scores, -jnp.inf)
        p = jax.nn.softmax(scores, axis=-1)
        o = jnp.einsum('bghts,bgsd->bghtd', p, v_all).reshape(Bx, H, Tx, HD)
        o = o.transpose(0, 2, 1, 3).reshape(Bx, Tx, H * HD)
        return jnp.einsum('bto,do->btd', o, Wo)

    def _L3_cond_ref(x, W, A, Bm, scalings, adapter_idx):
        import jax, jax.numpy as jnp
        import numpy as np
        B, T, D_IN, D_OUT = (16, 256, 256, 256)
        N_ADAPTERS, RANK = (8, 16)
        H = jnp.einsum('btd,od->bto', x, W)
        A_b = A[adapter_idx]
        B_b = Bm[adapter_idx]
        s_b = scalings[adapter_idx]
        xa = jnp.einsum('btd,brd->btr', x, A_b)
        delta = jnp.einsum('btr,bor->bto', xa, B_b)
        delta = jax.lax.stop_gradient(delta * s_b[:, None, None])
        return H + delta
    x = x + _L0_cond_ref(x, itok_B_0_7, L0_cond_weights, fside_8xS_0)
    x = x + _L1_cond_ref(x, itok_B_1_198, L1_cond_weights)
    x = x + _L2_cond_ref(x, L2_cond_Wq, L2_cond_Wk, L2_cond_Wv, L2_cond_Wo, L2_cond_q_norm_scale, L2_cond_k_norm_scale, L2_cond_k_blocks, L2_cond_v_blocks, itok_Bx257_0_4111, itok_B_37_3939)
    x = x + _L3_cond_ref(x, L3_cond_W, L3_cond_A, L3_cond_Bm, L3_cond_scalings, itok_B_0_6)
    return x

_drawn_inputs = setup_inputs


def setup_inputs(seed=0):
    import zlib

    import numpy as np

    out = dict(_drawn_inputs(seed))
    spreads = {'L3_cond_scalings': (1.0, 0.6)}
    factors = {'L2_cond_Wk': 55.244,
     'L2_cond_q_norm_scale': 8.0,
     'L2_cond_k_norm_scale': 200.0,
     'L2_cond_k_blocks': 4.217,
     'L3_cond_A': 3.13,
     'L3_cond_Bm': 3.16}
    for name, (base, spread) in spreads.items():
        noise = np.random.default_rng([zlib.crc32(name.encode()), seed]).standard_normal(out[name].shape)
        drawn = base * np.exp(spread * noise) if base else spread * noise
        out[name] = jnp.asarray(drawn.astype(out[name].dtype))
    for name, factor in factors.items():
        out[name] = (out[name] * factor).astype(out[name].dtype)
    return out
```

```python
import concourse.bass as bass
from concourse import mybir
from contextlib import ExitStack
import numpy as np

B, T, D = 32, 32, 256
TOK = B * T
NT = TOK // 128
BT = 128 // T
S0, S1 = 8, 200
H, G, HD = 8, 4, 32
BLK, WIN, NBLK = 16, 128, 257
NPOOL = 16 * NBLK
NSLOT = (WIN - 1 + T + BLK - 2) // BLK + 1
NKEY = NSLOT * BLK
HK = NKEY // 2
BR = 128 // NSLOT
RT = (B + BR - 1) // BR
RP = [min(BR, B - j * BR) * NSLOT for j in range(RT)]
NR = B * NSLOT
NA, RANK = 8, 16
SCALE = 256.0 ** -0.5
EPS = 1e-6
BIG = float(2.0 ** 100)
MAGIC = 1.5 * 2.0 ** 23
TWO_PI_HI = 6.28125
TWO_PI_LO = float(2 * np.pi - 6.28125)
PI_SAFE = 3.1415925

COLS_A = [("batch_in_tile", BT), ("channel", 1), ("read_batch", RT * B), ("slot", RT), ("read_row", RT),
          ("write_batch", B), ("half", 1), ("write_row", 1), ("offset", 8), ("code", 1), ("adapter", 1),
          ("index", 1), ("group_parity", 2), ("inv_freq", 16), ("half_sign", 32)]
COLS_B = [("ident", 128), ("iota", 128), ("later", 128), ("distance", NKEY), ("same_token", 128), ("merge", 64)]


def columns(table):
    at, out = 0, {}
    for name, n in table:
        out[name] = (at, at + n)
        at += n
    return out, at


AT_A, WA = columns(COLS_A)
AT_B, WB = columns(COLS_B)


def constants():
    p = np.arange(128)
    v = {}
    v["batch_in_tile"] = (p[:, None] // T == np.arange(BT)[None]).astype(np.float32)
    v["channel"] = (p % 32)[:, None]
    rb = np.arange(RT)[None] * BR + p[:, None] // NSLOT
    v["read_batch"] = (rb[:, :, None] == np.arange(B)[None, None]).reshape(128, -1)
    v["slot"] = np.repeat((p % NSLOT)[:, None], RT, 1)
    v["read_row"] = rb * NBLK
    wb = (p % 64) // 2
    v["write_batch"] = wb[:, None] == np.arange(B)[None]
    v["half"] = (p % 2)[:, None]
    v["write_row"] = (wb * NBLK)[:, None]
    v["offset"] = 2 * np.arange(8)[None] + (p // 64)[:, None]
    v["code"] = ((p // T) * 2 + (p % T) // 16)[:, None]
    v["adapter"] = (p // RANK)[:, None]
    v["index"] = p[:, None]
    v["group_parity"] = ((p // 32) % 2)[:, None] == np.arange(2)[None]
    inv = 1.0 / np.float32(10000.0) ** (np.arange(16, dtype=np.float32) / np.float32(16))
    v["inv_freq"] = np.repeat(inv[None].astype(np.float32), 128, 0)
    v["half_sign"] = np.repeat(np.where(np.arange(32) < 16, 1.0, -1.0)[None], 128, 0)
    v["ident"] = p[:, None] == p[None]
    v["iota"] = np.repeat(p[None], 128, 0)
    v["later"] = (p[None] > p[:, None]) & (p[None] // 64 == p[:, None] // 64)
    c = np.arange(NKEY)
    v["distance"] = (c % NSLOT * BLK + c // NSLOT)[None] - (p % T)[:, None]
    v["same_token"] = (p[:, None] % T) == (p[None] % T)
    v["merge"] = (p[:, None] % 64) == np.arange(64)[None]
    a = np.concatenate([v[n].astype(np.float32) for n, _ in COLS_A], 1)
    b = np.concatenate([v[n].astype(np.float32) for n, _ in COLS_B], 1)
    return np.ascontiguousarray(a), np.ascontiguousarray(b)


def build(nc, x, itok0, fside, itok1, table, kvlen, itok3, w0, w1, wq, wk, wv, wo, qscale, kscale,
          kblocks, vblocks, w3, a3, b3, scalings, const_a, const_b, out):
    f32, bf16, i32 = mybir.dt.float32, mybir.dt.bfloat16, mybir.dt.int32
    ALU, ACT, AX = mybir.AluOpType, mybir.ActivationFunctionType, mybir.AxisListType

    x_rows = x.rearrange("(n b) t d -> (b t) n d", b=BT)
    out_rows = out.rearrange("(n b) t d -> (b t) n d", b=BT)
    table_rows = table.rearrange("b (n o) -> (b n) o", o=1)
    w0_rows = w0.rearrange("s c d -> (s c) d")
    w1_rows = w1.rearrange("s c d -> (s c) d")
    k_rows = kblocks.rearrange("n g o d -> n (g o d)")
    v_rows = vblocks.rearrange("n g o d -> n (g o d)")

    ctx = ExitStack()
    with ctx:
        def sb(name, shape, dt=f32):
            return ctx.enter_context(nc.sbuf_tensor(name, shape, dt))

        def sem(name):
            return ctx.enter_context(nc.semaphore(name))

        ca = sb("ca", [128, WA])
        cb = sb("cb", [128, WB])

        def A_(name):
            return ca[:, AT_A[name][0]:AT_A[name][1]]

        def B_(name):
            return cb[:, AT_B[name][0]:AT_B[name][1]]

        ident = B_("ident")
        ones = sb("ones", [128, 128])
        spread = sb("spread", [128, BT, 128], bf16)
        vec_i = sb("vec_i", [128, 4, B], i32)
        vec = sb("vec", [128, 4, B])
        pick4 = sb("pick4", [128, 4, NT, BT])
        tokv = sb("tokv", [128, 4, NT])
        idx01f = sb("idx01f", [128, 2, NT])
        idx01 = sb("idx01", [128, 2, NT], i32)
        rtmp = sb("rtmp", [128, RT, B])
        rkv = sb("rkv", [128, 4, RT])
        ridx = sb("ridx", [128, RT], i32)
        rblk_i = sb("rblk_i", [128, RT], i32)
        rblk = sb("rblk", [128, RT])
        wtmp = sb("wtmp", [128, B])
        wkv = sb("wkv", [128, 8])
        widx = sb("widx", [128, 2], i32)
        wtab_i = sb("wtab_i", [128, 2], i32)
        wtab = sb("wtab", [128, 4])
        wrap = sb("wrap", [128, 8])
        wblk = sb("wblk", [128, 8])
        wlive = sb("wlive", [128, 8])
        dead = sb("dead", [128, 8])
        hot = sb("hot", [S0, B])
        bias_all = sb("bias_all", [128, NT, BT])
        bias = sb("bias", [128, NT])
        tok = sb("tok", [128, 6, NT])
        pos = sb("pos", [128, 2 * NT])
        trig = sb("trig", [128, 2, 2 * NT, 16])
        nscale = sb("nscale", [128, 2, HD])
        nsign = sb("nsign", [128, 2, HD])
        rope_c = sb("rope_c", [128, 2 * NT, HD])
        rope_s = sb("rope_s", [128, 2 * NT, HD])
        dist = sb("dist", [128, 2, NKEY])
        maskb = sb("maskb", [128, NT, NKEY], bf16)
        fside_sb = sb("fside_sb", [S0, BT, HD])
        scal = sb("scal", [128, 1])
        amask = sb("amask", [128, B])
        wg = sb("wg", [128, 2, NT, 32])
        xs = sb("xs", [128, NT, D])
        kz = sb("kz", [128, RT, BLK * 128])
        early = kz[:, :, :].rearrange("p j n -> p (j n)")
        bd = early[:, 0:2048].rearrange("p (m n q) -> p m n q", m=2, n=NT)
        wq_sb = early[:, 2048:2560].rearrange("p (h d) -> p h d", h=2)
        wkv_sb = early[:, 2560:3072].rearrange("p (h d) -> p h d", h=2)
        w3_sb = early[:, 3072:3584].rearrange("p (h d) -> p h d", h=2)
        a3_sb = early[:, 3584:3840]
        b3_sb = early[:, 3840:4096].rearrange("p (h a r) -> p h a r", h=2, a=NA)
        wo_sb = early[:, 4096:4608].rearrange("p (o h e) -> p o h e", o=2, h=2)
        ang = early[:, 4608:4864].rearrange("p (n i) -> p n i", n=2 * NT)
        turn = early[:, 4864:5376].rearrange("p (k n i) -> p k n i", k=2, n=2 * NT)
        red = early[:, 5376:5888].rearrange("p (k n i) -> p k n i", k=2, n=2 * NT)
        wqkvT = sb("wqkvT", [128, 2, 512])
        w3T = sb("w3T", [128, 2, D])
        abT = sb("abT", [128, 512])
        woT = sb("woT", [128, 2, D])
        zs = sb("zs", [128, 2, 384])
        sq = sb("sq", [128, 2, 384])
        ra = sb("ra", [128, 12, HD])
        rb = sb("rb", [128, 12, HD])
        ss = sb("ss", [128, 4, 12])
        qr = sb("qr", [128, 2, D])
        new = sb("new", [128, 8, 2, 128])
        QT = sb("QT", [128, B, 2 * T])
        kraw = sb("kraw", [128, RT, BLK * 128])
        vraw = sb("vraw", [128, RT, BLK * 128])
        keep = sb("keep", [128, RT, BLK])
        OH = sb("OH", [128, 8, NR])
        KT = sb("KT", [128, B, NKEY])
        VT = sb("VT", [128, B, NKEY])
        kt = KT[:, :, :].rearrange("p b c -> p (b c)")
        xT = kt[:, 0:2048].rearrange("p (c t) -> p c t", c=2)
        xTo = kt[:, 2048:4096].rearrange("p (c o b i) -> p c o b i", c=2, o=BLK, b=B)
        perm = kt[:, 4096:5120].rearrange("p (n q) -> p n q", n=NT)
        vflat = VT[:, :, :].rearrange("p b c -> p (b c)")
        diag_w = vflat[:, 0:1024].rearrange("p (j q) -> p j q", j=8)
        wrow = vflat[:, 1024:2048]
        eq = vflat[:, 2048:3072]
        diag_r = vflat[:, 3072:3456].rearrange("p (j q) -> p j q", j=3)
        rrow = vflat[:, 3456:3456 + NR]
        vz = kraw
        NQB = 4
        QB = early[:, 0:NQB * 1024].rearrange("p (k b g q) -> p k b g q", k=NQB, b=BT, g=2)
        kflat = vraw[:, :, :].rearrange("p j n -> p (j n)")

        def carve(at, n):
            return kflat[:, at:at + n], at + n

        P_, at = carve(0, 3 * 2 * NKEY)
        P = P_.rearrange("p (k g c) -> p k g c", k=3, g=2)
        PT_, at = carve(at, 2 * 512)
        PT = PT_.rearrange("p (k n) -> p k n", k=2)
        V2_, at = carve(at, 4 * 256)
        V2 = V2_.rearrange("p (k n) -> p k n", k=4)
        osb = sb("osb", [128, BT, 2, 2, HD])
        oT = sb("oT", [128, 2, 128])
        x3T = sb("x3T", [128, 2, 128])
        xam = sb("xam", [128, 128])
        nmax = sb("nmax", [128, B, 2])
        rsum = sb("rsum", [128, B, 2])
        rinv = sb("rinv", [128, B, 2])

        bank = [ctx.enter_context(nc.psum_tensor(f"bank{i}", [128, 512], f32)) for i in range(8)]

        s_vec = sem("s_vec")
        s_ca = sem("s_ca")
        s_cb = sem("s_cb")
        s_x = [sem("s_x0"), sem("s_x1")]
        s_small = sem("s_small")
        s_wqkv = sem("s_wqkv")
        s_w3 = sem("s_w3")
        s_wo = sem("s_wo")
        s_g0 = sem("s_g0")
        s_g1 = sem("s_g1")
        s_rt = sem("s_rt")
        s_wt = sem("s_wt")
        s_k = sem("s_k")
        s_v = sem("s_v")
        s_out = sem("s_out")

        v_idx01 = sem("v_idx01")
        v_idxt = sem("v_idxt")
        v_ridx = sem("v_ridx")
        v_hot = sem("v_hot")
        v_perm = sem("v_perm")
        v_bd = sem("v_bd")
        v_angles = sem("v_angles")
        v_mask = sem("v_mask")
        v_diag = sem("v_diag")
        v_oh = sem("v_oh")
        v_keep = sem("v_keep")
        v_x1 = sem("v_x1")
        v_x2 = sem("v_x2")
        v_xto = sem("v_xto")
        v_zread = sem("v_zread")
        v_sqread = sem("v_sqread")
        v_ms = sem("v_ms")
        v_mid = sem("v_mid")
        v_dist = sem("v_dist")
        v_rope = sem("v_rope")
        v_t1 = sem("v_t1")
        v_max = sem("v_max")
        v_v2 = sem("v_v2")
        v_osb = sem("v_osb")
        v_ot = sem("v_ot")
        v_x3 = sem("v_x3")
        v_x3t = sem("v_x3t")
        v_xam = sem("v_xam")
        v_fin = sem("v_fin")
        v_chain = sem("v_chain")

        g_ones = sem("g_ones")
        g_zk = sem("g_zk")
        g_zv = sem("g_zv")
        g_qb = sem("g_qb")

        a_wt = sem("a_wt")
        a_same = sem("a_same")
        a_trig = sem("a_trig")
        a_wrow = sem("a_wrow")
        a_xt = sem("a_xt")
        a_sq = sem("a_sq")
        a_root = sem("a_root")
        a_z = sem("a_z")
        a_dist = sem("a_dist")
        a_qt = sem("a_qt")
        a_t1 = sem("a_t1")
        a_exp = sem("a_exp")
        a_pt = sem("a_pt")

        p_wt = sem("p_wt")
        p_bias = sem("p_bias")
        p_l0 = sem("p_l0")
        p_l1 = sem("p_l1")
        p_xt = sem("p_xt")
        p_idx = sem("p_idx")
        p_z = sem("p_z")
        p_qt = sem("p_qt")
        p_t1 = sem("p_t1")
        p_s = sem("p_s")
        p_v2 = sem("p_v2")
        p_pt = sem("p_pt")
        p_o = sem("p_o")
        p_ot = sem("p_ot")
        p_y = sem("p_y")
        p_x3t = sem("p_x3t")
        p_xa = sem("p_xa")
        p_h = sem("p_h")

        WT_BANK = [0, 1]
        L0_BANK = [3, 4]
        L1_BANK = [5, 6]
        XT_BANK = [7, 2]
        XTO_BANK = [3, 4]
        Z_BANK = [4, 5, 6]
        QT_BANK = [0, 1]
        T1_BANK = [2, 3, 7, 4, 5, 6]
        S_BANK = [0, 1, 2]
        PT_BANK = [3, 4]
        V2_BANK, O_BANK, TAIL_BANK = 5, 6, 7
        NT1 = 2 * BLK

        def t1_dst(k):
            return (KT if k < BLK else VT)[:, :, NSLOT * (k % BLK):NSLOT * (k % BLK) + NSLOT]

        def t1_src(k):
            return bank[T1_BANK[k % 6]][:, 0:NR].rearrange("p (b s) -> p b s", b=B)

        block = ctx.enter_context(nc.Block())

        @block.sync
        def _(sp):
            for n, v in enumerate((itok0, itok1, kvlen, itok3)):
                sp.dma_start(vec_i[:, n, :], v.partition_broadcast(128)).then_inc(s_vec, 16)
            sp.dma_start(ca[:, :], const_a).then_inc(s_ca, 16)
            sp.dma_start(cb[:, :], const_b).then_inc(s_cb, 16)
            sp.dma_start(xs[:, 0:4, :], x_rows[:, 0:4, :]).then_inc(s_x[0], 16)
            sp.dma_start(wq_sb[:, :, :], wq.rearrange("(h o) d -> o h d", o=128)).then_inc(s_wqkv, 16)
            sp.dma_start(wkv_sb[:, 0, :], wk).then_inc(s_wqkv, 16)
            sp.dma_start(wkv_sb[:, 1, :], wv).then_inc(s_wqkv, 16)
            sp.dma_start(xs[:, 4:8, :], x_rows[:, 4:8, :]).then_inc(s_x[1], 16)
            sp.dma_start(fside_sb[:, :, :], fside.rearrange("s (a d) -> s a d", a=1).broadcast_to([S0, BT, HD]))\
                .then_inc(s_small, 16)
            sp.dma_start(nscale[:, 0, :], qscale.partition_broadcast(128)).then_inc(s_small, 16)
            sp.dma_start(nscale[:, 1, :], kscale.partition_broadcast(128)).then_inc(s_small, 16)
            for a in range(NA):
                sp.dma_start(scal[RANK * a:RANK * (a + 1), :], scalings[a:a + 1].partition_broadcast(RANK))\
                    .then_inc(s_small, 16)
            sp.dma_start(w3_sb[:, :, :], w3.rearrange("(h o) d -> o h d", o=128)).then_inc(s_w3, 16)
            sp.dma_start(a3_sb[:, :], a3.rearrange("a r d -> (a r) d")).then_inc(s_w3, 16)
            for h in range(2):
                sp.dma_start(b3_sb[:, h, :, :], b3[:, 128 * h:128 * h + 128, :].rearrange("a o r -> o a r"))\
                    .then_inc(s_w3, 16)
            for o in range(2):
                for h in range(2):
                    sp.dma_start(wo_sb[:, o, h, :].rearrange("p (g d) -> p g d", g=G),
                                 wo[128 * o:128 * o + 128, :].rearrange("o (g h d) -> h o g d", g=G, h=2)[h])\
                        .then_inc(s_wo, 16)
            for n in range(NT):
                sp.wait_ge(v_fin, n + 1)
                sp.dma_start(out_rows[:, n, :], xs[:, n, :]).then_inc(s_out, 16)
            sp.wait_ge(s_out, 16 * NT)

        @block.gpsimd
        def _(pool):
            pool.memset(ones[:, :], 1.0).then_inc(g_ones, 1)
            pool.memset(osb[:, :, :, :, :], 0.0).then_inc(g_ones, 1)

            def gather(dst, src, idx, done):
                pool.indirect_dma_start(out=dst, out_offset=None, in_=src,
                                        in_offset=bass.IndirectOffsetOnAxis(ap=idx, axis=0)).then_inc(done, 16)

            pool.wait_ge(v_idx01, 1)
            for n in range(NT):
                gather(wg[:, 0, n, :], w0_rows, idx01[:, 0, n:n + 1], s_g0)
            pool.wait_ge(v_idxt, 1)
            for j in range(RT):
                gather(rblk_i[0:RP[j], j:j + 1], table_rows, ridx[0:RP[j], j:j + 1], s_rt)
            for j in range(2):
                gather(wtab_i[:, j:j + 1], table_rows, widx[:, j:j + 1], s_wt)
            for n in range(NT):
                gather(wg[:, 1, n, :], w1_rows, idx01[:, 1, n:n + 1], s_g1)
            pool.wait_ge(s_rt, 16 * RT)
            for j in range(RT):
                gather(kraw[0:RP[j], j, :], k_rows, rblk_i[0:RP[j], j:j + 1], s_k)
            for j in range(RT):
                gather(vraw[0:RP[j], j, :], v_rows, rblk_i[0:RP[j], j:j + 1], s_v)
            pool.wait_ge(v_keep, 1)
            for raw, dst, landed, done in ((kraw, kz, s_k, g_zk), (vraw, vz, s_v, g_zv)):
                pool.wait_ge(landed, 16 * RT)
                for j in range(RT):
                    if dst is vz:
                        pool.wait_ge(g_zk, j + 1)
                    pool.tensor_tensor(dst[0:RP[j], j, :].rearrange("p (o g d) -> p g o d", g=G, o=BLK),
                                       raw[0:RP[j], j, :].rearrange("p (g o d) -> p g o d", g=G, o=BLK),
                                       keep[0:RP[j], j, :].unsqueeze(1).unsqueeze(3)
                                       .broadcast_to([RP[j], G, BLK, HD]), ALU.mult).then_inc(done, 1)

            pool.wait_ge(a_qt, NT)
            pool.wait_ge(p_t1, BLK)
            for n in range(NT):
                if n >= NQB:
                    pool.wait_ge(p_s, BT * (n - NQB + 1))
                for g in range(G):
                    src = QT[:, BT * n:BT * n + BT, :]
                    pool.tensor_scalar(QB[:, n % NQB, :, g // 2, 64 * (g % 2):64 * (g % 2) + 64], src,
                                       A_("batch_in_tile")[:, g:g + 1], None, ALU.mult).then_inc(g_qb, 1)

        @block.scalar
        def _(act):
            act.wait_ge(s_ca, 16)
            act.wait_ge(s_cb, 16)
            for b in range(BT):
                nc.scalar.activation(spread[:, b, :], B_("same_token"), ACT.Copy,
                                     scale=A_("batch_in_tile")[:, b:b + 1]).then_inc(a_same, 1)
            wt_dst = [wqkvT[:, :, 0:256], wqkvT[:, :, 256:512], w3T[:, :, :], abT[:, :], woT[:, :, :]]
            for k in range(2):
                act.wait_ge(p_wt, k + 1)
                nc.scalar.activation(wt_dst[k], bank[WT_BANK[k % 2]][:, :].rearrange("p (c n) -> p c n", c=2),
                                     ACT.Copy).then_inc(a_wt, 1)
            act.wait_ge(v_angles, 1)
            nc.scalar.activation(trig[:, :, :, :], red[:, :, :, :], ACT.Sin).then_inc(a_trig, 1)
            for n in range(NT):
                act.wait_ge(p_xt, n + 1)
                z = bank[XT_BANK[n % 2]][:, 0:256].rearrange("p (c t) -> p c t", c=2)
                nc.scalar.activation(xT[:, :, 128 * n:128 * n + 128], z, ACT.Copy).then_inc(a_xt, 1)
            for k in range(2, 5):
                act.wait_ge(p_wt, k + 1)
                src = bank[WT_BANK[k % 2]][:, :]
                if k != 3:
                    src = src.rearrange("p (c n) -> p c n", c=2)
                nc.scalar.activation(wt_dst[k], src, ACT.Copy).then_inc(a_wt, 1)
            act.wait_ge(p_idx, 1)
            for h in range(2):
                nc.scalar.activation(wrow[:, 512 * h:512 * h + 512], bank[h][:, :], ACT.Copy).then_inc(a_wrow, 1)
            nc.scalar.activation(rrow, bank[3][:, 0:NR], ACT.Copy).then_inc(a_wrow, 1)

            def queries_out(n):
                act.wait_ge(p_qt, n + 1)
                src = bank[QT_BANK[n % 2]][:, 0:256].rearrange("p (h b t) -> p b h t", h=2, b=BT)
                dst = QT[:, BT * n:BT * n + BT, :].rearrange("p b (h t) -> p b h t", h=2)
                nc.scalar.activation(dst, src, ACT.Copy).then_inc(a_qt, 1)

            for n in range(NT):
                act.wait_ge(p_z, n + 1)
                if n >= 2:
                    act.wait_ge(v_sqread, n - 1)
                z = bank[Z_BANK[n % 3]]
                if n >= 2:
                    act.wait_ge(v_zread, n - 1)
                nc.scalar.activation(zs[:, n % 2, :], z[:, 0:384], ACT.Copy).then_inc(a_z, 1)
                nc.scalar.activation(new[:, n, 1, :], z[:, 384:512], ACT.Copy).then_inc(a_z, 1)
                act.wait_ge(a_z, 2 * n + 1)
                nc.scalar.activation(sq[:, n % 2, :], zs[:, n % 2, :], ACT.Square).then_inc(a_sq, 1)
                act.wait_ge(v_ms, n + 1)
                nc.scalar.activation(ss[:, 2, :], ss[:, 1, :], ACT.Sqrt).then_inc(a_root, 1)
                if n >= 2:
                    queries_out(n - 2)
            queries_out(NT - 2)
            queries_out(NT - 1)
            act.wait_ge(v_mid, 1)
            for n in range(NT):
                if n >= 2:
                    act.wait_ge(v_dist, n - 1)
                nc.scalar.activation(dist[:, n % 2, :], B_("distance"), ACT.Square, bias=tok[:, 5, n:n + 1])\
                    .then_inc(a_dist, 1)
            for k in range(1, NT1, 2):
                act.wait_ge(p_t1, k + 1)
                nc.scalar.activation(t1_dst(k), t1_src(k), ACT.Copy).then_inc(a_t1, 1)

            def pt_out(b):
                act.wait_ge(p_pt, b + 1)
                if b >= 2:
                    act.wait_ge(p_o, b - 1)
                nc.scalar.activation(PT[0:HK, b % 2, :], bank[PT_BANK[b % 2]][0:HK, :], ACT.Copy).then_inc(a_pt, 1)

            for i in range(B + 2):
                if i < B:
                    act.wait_ge(v_max, i + 1)
                    if i >= 3:
                        act.wait_ge(p_pt, i - 2)
                    for g in range(2):
                        nc.scalar.activation(P[:, i % 3, g, :], bank[S_BANK[i % 3]][:, NKEY * g:NKEY * g + NKEY],
                                             ACT.Exp, bias=nmax[:, i, g:g + 1], scale=SCALE,
                                             accum_out=rsum[:, i, g:g + 1]).then_inc(a_exp, 1)
                if i >= 2:
                    pt_out(i - 2)

        @block.vector
        def _(dve):
            V = nc.vector
            chain = [0]

            def link(ins):
                chain[0] += 1
                ins.then_inc(v_chain, 1)
                dve.wait_ge(v_chain, chain[0])

            def blocks_of(dst, src):
                link(V.tensor_scalar(dst, src, (1.0 - BLK) / 2, 1.0 / BLK, ALU.add, ALU.mult))
                link(V.tensor_scalar(dst, dst, MAGIC, None, ALU.add))
                link(V.tensor_scalar(dst, dst, MAGIC, None, ALU.subtract))

            dve.wait_ge(s_vec, 64)
            dve.wait_ge(s_ca, 16)
            link(V.tensor_copy(vec[:, :, :], vec_i[:, :, :]))
            link(V.tensor_tensor(pick4[:, :, :, :], vec[:, :, :].rearrange("p v (n b) -> p v n b", b=BT),
                                 A_("batch_in_tile").unsqueeze(1).unsqueeze(1).broadcast_to([128, 4, NT, BT]),
                                 ALU.mult))
            link(V.tensor_reduce(tokv[:, :, :], pick4[:, :, :, :], AX.X, ALU.add))
            link(V.tensor_scalar(idx01f[:, :, :], tokv[:, 0:2, :], 32.0, A_("channel"), ALU.mult, ALU.add))
            V.tensor_copy(idx01[:, :, :], idx01f[:, :, :]).then_inc(v_idx01, 1)
            link(V.tensor_tensor(rtmp[:, :, :], A_("read_batch").rearrange("p (j b) -> p j b", j=RT),
                                 vec[:, 2, :].unsqueeze(1).broadcast_to([128, RT, B]), ALU.mult))
            link(V.tensor_reduce(rkv[:, 0, :], rtmp[:, :, :], AX.X, ALU.add))
            link(V.tensor_scalar(rkv[:, 1, :], rkv[:, 0, :], float(1 - WIN), 0.0, ALU.add, ALU.max))
            blocks_of(rkv[:, 2, :], rkv[:, 1, :])
            link(V.tensor_tensor(rkv[:, 0, :], rkv[:, 2, :], A_("slot"), ALU.add))
            V.tensor_tensor(ridx[:, :], rkv[:, 0, :], A_("read_row"), ALU.add)
            link(V.tensor_tensor(wtmp[:, :], A_("write_batch"), vec[:, 2, :], ALU.mult))
            link(V.tensor_reduce(wkv[:, 0:1], wtmp[:, :], AX.X, ALU.add))
            blocks_of(wkv[:, 2:3], wkv[:, 0:1])
            link(V.scalar_tensor_tensor(wkv[:, 1:2], wkv[:, 2:3], float(-BLK), wkv[:, 0:1], ALU.mult, ALU.add))
            link(V.tensor_tensor(wkv[:, 3:4], wkv[:, 2:3], A_("half"), ALU.add))
            link(V.tensor_tensor(wkv[:, 4:5], wkv[:, 3:4], A_("write_row"), ALU.add))
            V.tensor_copy(widx[:, 0:1], wkv[:, 4:5])
            V.tensor_scalar(widx[:, 1:2], wkv[:, 4:5], 1.0, None, ALU.add).then_inc(v_idxt, 1)
            V.tensor_scalar(hot[:, :], vec[0:S0, 0, :], A_("index")[0:S0, :], None, ALU.is_equal).then_inc(v_hot, 1)
            link(V.tensor_scalar(tok[:, 0, :], tokv[:, 2, :], A_("channel"), None, ALU.add))
            blocks_of(tok[:, 2, :], tok[:, 0, :])
            link(V.scalar_tensor_tensor(tok[:, 1, :], tok[:, 2, :], float(-BLK), tok[:, 0, :], ALU.mult, ALU.add))
            link(V.tensor_scalar(tok[:, 2, :], tok[:, 1, :], 8.0, A_("code"), ALU.mult, ALU.add))
            dve.wait_ge(s_cb, 16)
            for n in range(NT):
                V.tensor_scalar(perm[:, n, :], B_("iota"), tok[:, 2, n:n + 1], None, ALU.is_equal).then_inc(v_perm, 1)

            def block_diagonal(m, arrived):
                dve.wait_ge(arrived, 16 * NT)
                V.tensor_tensor(bd[:, m, :, :].rearrange("p n (b d) -> p n b d", b=BT),
                                wg[:, m, :, :].unsqueeze(2).broadcast_to([128, NT, BT, 32]),
                                A_("batch_in_tile").unsqueeze(1).unsqueeze(3).broadcast_to([128, NT, BT, 32]),
                                ALU.mult).then_inc(v_bd, 1)

            block_diagonal(0, s_g0)
            dve.wait_ge(p_bias, 1)
            link(V.tensor_tensor(bias_all[:, :, :], bank[2][:, 0:B].rearrange("p (n b) -> p n b", b=BT),
                                 A_("batch_in_tile").unsqueeze(1).broadcast_to([128, NT, BT]), ALU.mult))
            link(V.tensor_reduce(bias[:, :], bias_all[:, :, :], AX.X, ALU.add))
            for g in range(4):
                dve.wait_ge(p_l0, g + 1)
                for n in (2 * g, 2 * g + 1):
                    V.scalar_tensor_tensor(xs[:, n, :], bank[L0_BANK[g % 2]][:, 256 * (n % 2):256 * (n % 2) + 256],
                                           bias[:, n:n + 1], xs[:, n, :], ALU.add, ALU.add).then_inc(v_x1, 1)
            block_diagonal(1, s_g1)
            V.tensor_scalar(wrap[:, :], A_("offset"), wkv[:, 1:2], None, ALU.is_lt)
            V.tensor_copy(pos[:, 0:NT], tok[:, 0, :])
            link(V.tensor_scalar(wkv[:, 5:6], wkv[:, 3:4], float(BLK), None, ALU.mult))
            link(V.scalar_tensor_tensor(pos[:, NT:2 * NT], wrap[:, :], float(BLK), A_("offset"), ALU.mult, ALU.add))
            link(V.tensor_scalar(pos[:, NT:2 * NT], pos[:, NT:2 * NT], wkv[:, 5:6], None, ALU.add))
            link(V.tensor_tensor(ang[:, :, :], pos[:, :].unsqueeze(2).broadcast_to([128, 2 * NT, 16]),
                                 A_("inv_freq").unsqueeze(1).broadcast_to([128, 2 * NT, 16]), ALU.mult))
            for k in range(2):
                link(V.tensor_scalar(turn[:, k, :, :], ang[:, :, :], float(1 / (2 * np.pi)), 0.25 * k,
                                     ALU.mult, ALU.add))
            link(V.tensor_scalar(turn[:, :, :, :], turn[:, :, :, :], MAGIC, None, ALU.add))
            link(V.tensor_scalar(turn[:, :, :, :], turn[:, :, :, :], MAGIC, None, ALU.subtract))
            for k in range(2):
                link(V.scalar_tensor_tensor(red[:, k, :, :], turn[:, k, :, :], -TWO_PI_HI, ang[:, :, :],
                                            ALU.mult, ALU.add))
            link(V.scalar_tensor_tensor(red[:, :, :, :], turn[:, :, :, :], -TWO_PI_LO, red[:, :, :, :],
                                        ALU.mult, ALU.add))
            link(V.tensor_scalar(red[:, 1, :, :], red[:, 1, :, :], float(np.pi / 2), None, ALU.add))
            V.tensor_scalar(red[:, :, :, :], red[:, :, :, :], PI_SAFE, -PI_SAFE, ALU.min, ALU.max)\
                .then_inc(v_angles, 1)
            for g in range(4):
                dve.wait_ge(p_l1, g + 1)
                V.tensor_tensor(xs[:, 2 * g:2 * g + 2, :],
                                bank[L1_BANK[g % 2]][:, :].rearrange("p (n d) -> p n d", n=2),
                                xs[:, 2 * g:2 * g + 2, :], ALU.add).then_inc(v_x2, 1)
            dve.wait_ge(s_small, 16 * (3 + NA))
            dve.wait_ge(a_trig, 1)
            link(V.tensor_scalar(nscale[:, :, :], nscale[:, :, :], 1.0, float(HD) ** 0.5, ALU.add, ALU.mult))
            link(V.tensor_tensor(nsign[:, :, :], nscale[:, :, :],
                                 A_("half_sign").unsqueeze(1).broadcast_to([128, 2, HD]), ALU.mult))
            for k in range(2):
                t = slice(NT * k, NT * k + NT)
                for f, (dst, sc) in enumerate(((rope_s, nsign), (rope_c, nscale))):
                    last = V.tensor_tensor(
                        dst[:, t, :].rearrange("p n (h i) -> p n h i", h=2),
                        trig[:, f, t, :].unsqueeze(2).broadcast_to([128, NT, 2, 16]),
                        sc[:, k, :].rearrange("p (h i) -> p h i", h=2).unsqueeze(1).broadcast_to([128, NT, 2, 16]),
                        ALU.mult)
            link(last)

            dve.wait_ge(s_wt, 32)
            dve.wait_ge(s_rt, 16 * RT)
            link(V.tensor_copy(wtab[:, 0:2], wtab_i[:, :]))
            link(V.tensor_tensor(wtab[:, 2:3], wtab[:, 1:2], wtab[:, 0:1], ALU.subtract))
            link(V.tensor_scalar(wblk[:, :], wrap[:, :], wtab[:, 2:3], wtab[:, 0:1], ALU.mult, ALU.add))
            V.tensor_tensor(diag_w, ident.unsqueeze(1).broadcast_to([128, 8, 128]),
                            wblk[:, :].unsqueeze(2).broadcast_to([128, 8, 128]), ALU.mult)
            for j in range(RT):
                link(V.tensor_copy(rblk[0:RP[j], j:j + 1], rblk_i[0:RP[j], j:j + 1]))
                V.tensor_scalar(diag_r[0:RP[j], j, 0:RP[j]], ident[0:RP[j], 0:RP[j]], rblk[0:RP[j], j:j + 1], None,
                                ALU.mult).then_inc(v_diag, 1)
            for n in range(NT):
                dve.wait_ge(p_xt, n + 1)
                dst = xTo[:, :, :, BT * n:BT * n + BT, :].rearrange("p c o b i -> p c o (b i)")
                src = bank[XTO_BANK[n % 2]][:, 0:256].rearrange("p (c o e) -> p c o e", c=2, o=BLK)
                V.tensor_copy(dst, src).then_inc(v_xto, 1)
            dve.wait_ge(a_wrow, 3)
            eq3 = eq.rearrange("p (j q) -> p j q", j=8)
            link(V.tensor_tensor(eq3, wrow.rearrange("p (j q) -> p j q", j=8),
                                 wblk[:, :].unsqueeze(2).broadcast_to([128, 8, 128]), ALU.is_equal))
            link(V.tensor_tensor(eq3, eq3, B_("later").unsqueeze(1).broadcast_to([128, 8, 128]), ALU.mult))
            link(V.tensor_reduce(dead[:, :], eq3, AX.X, ALU.max))
            link(V.scalar_tensor_tensor(wlive[:, :], dead[:, :], -10000.0, wblk[:, :], ALU.mult, ALU.add))
            for j in range(8):
                V.tensor_scalar(OH[:, j, :], rrow, wlive[:, j:j + 1], None, ALU.is_equal).then_inc(v_oh, 1)
            for j in range(RT):
                link(V.tensor_scalar(eq[0:RP[j], :], wrow[0:RP[j], :], rblk[0:RP[j], j:j + 1], None, ALU.is_equal))
                link(V.tensor_reduce(keep[0:RP[j], j, :], eq[0:RP[j], :].rearrange("p (o q) -> p o q", o=BLK), AX.X,
                                     ALU.max))
                kept = V.tensor_scalar(keep[0:RP[j], j, :], keep[0:RP[j], j, :], -1.0, 1.0, ALU.mult, ALU.add)
                if j < RT - 1:
                    link(kept)
            kept.then_inc(v_keep, 1)
            for n in range(NT):
                dve.wait_ge(a_z, 2 * n + 1)
                if n >= 1:
                    dve.wait_ge(v_rope, 2 * n)
                zq = zs[:, n % 2, 0:256].rearrange("p (h d) -> p h d", h=H)
                zk = zs[:, n % 2, 256:384].rearrange("p (h d) -> p h d", h=G)
                V.tensor_tensor(ra[:, 0:H, :], zq, rope_c[:, n, :].unsqueeze(1).broadcast_to([128, H, HD]), ALU.mult)
                V.tensor_tensor(ra[:, H:12, :], zk, rope_c[:, NT + n, :].unsqueeze(1).broadcast_to([128, G, HD]),
                                ALU.mult)
                V.tensor_tensor(rb[:, 0:H, :], zq, rope_s[:, n, :].unsqueeze(1).broadcast_to([128, H, HD]), ALU.mult)
                V.tensor_tensor(rb[:, H:12, :], zk, rope_s[:, NT + n, :].unsqueeze(1).broadcast_to([128, G, HD]),
                                ALU.mult).then_inc(v_zread, 1)
                dve.wait_ge(v_zread, n + 1)
                dve.wait_ge(a_sq, n + 1)
                V.tensor_reduce(ss[:, 0, :], sq[:, n % 2, :].rearrange("p (h d) -> p h d", h=12), AX.X,
                                ALU.add).then_inc(v_sqread, 1)
                dve.wait_ge(v_sqread, n + 1)
                V.tensor_scalar(ss[:, 1, :], ss[:, 0, :], HD * EPS, None, ALU.add).then_inc(v_ms, 1)
                link(V.tensor_tensor(ra[:, :, :].rearrange("p h (k i) -> p h k i", k=2),
                                     ra[:, :, :].rearrange("p h (k i) -> p h k i", k=2),
                                     rb[:, :, :].rearrange("p h (k i) -> p h k i", k=2)[:, :, ::-1, :], ALU.add))
                dve.wait_ge(a_root, n + 1)
                link(V.reciprocal(ss[:, 3, :], ss[:, 2, :]))
                if n >= 2:
                    dve.wait_ge(p_qt, n - 1)
                V.tensor_tensor(qr[:, n % 2, :].rearrange("p (h g d) -> p g h d", h=2, g=G),
                                ra[:, 0:H, :].rearrange("p (g h) d -> p g h d", h=2),
                                ss[:, 3, 0:H].rearrange("p (g h) -> p g h", h=2).unsqueeze(3)
                                .broadcast_to([128, G, 2, HD]), ALU.mult).then_inc(v_rope, 1)
                V.tensor_tensor(new[:, n, 0, :].rearrange("p (h d) -> p h d", h=G), ra[:, H:12, :],
                                ss[:, 3, H:12].unsqueeze(2).broadcast_to([128, G, HD]), ALU.mult).then_inc(v_rope, 1)
            link(V.tensor_scalar(tok[:, 1, :], tokv[:, 2, :], float(1 - WIN), 0.0, ALU.add, ALU.max))
            blocks_of(tok[:, 3, :], tok[:, 1, :])
            link(V.scalar_tensor_tensor(tok[:, 4, :], tok[:, 3, :], float(BLK), tokv[:, 2, :], ALU.mult, ALU.subtract))
            V.tensor_scalar(tok[:, 5, :], tok[:, 4, :], WIN / 2 - 0.5, None, ALU.add).then_inc(v_mid, 1)
            for n in range(NT):
                dve.wait_ge(a_dist, n + 1)
                V.tensor_scalar(maskb[:, n, :], dist[:, n % 2, :], (WIN / 2) ** 2, -BIG, ALU.is_gt, ALU.mult)\
                    .then_inc(v_dist, 1)
            V.tensor_scalar(amask[:, :], vec[:, 3, :], A_("adapter"), scal[:, 0:1], ALU.is_equal, ALU.mult)\
                .then_inc(v_mask, 1)
            for k in range(0, NT1, 2):
                dve.wait_ge(p_t1, k + 1)
                V.tensor_copy(t1_dst(k), t1_src(k)).then_inc(v_t1, 1)

            tail = bank[TAIL_BANK]

            def normalise(n):
                dve.wait_ge(p_o, BT * n + BT)
                if n >= 1:
                    dve.wait_ge(p_ot, n)
                else:
                    dve.wait_ge(g_ones, 2)
                link(V.reciprocal(rinv[:, BT * n:BT * n + BT, :], rsum[:, BT * n:BT * n + BT, :]))
                for g in range(2):
                    p = slice(64 * g, 64 * g + 64)
                    V.tensor_tensor(osb[p, :, :, g, :],
                                    bank[O_BANK][p, :].rearrange("p (b k e) -> p b k e", b=BT, k=2)
                                    [:, :, :, HD * g:HD * g + HD],
                                    rinv[p, BT * n:BT * n + BT, :].unsqueeze(3).broadcast_to([64, BT, 2, HD]),
                                    ALU.mult).then_inc(v_osb, 1)

            def steps(n):
                def s_norm():
                    normalise(n)

                def s_ot():
                    dve.wait_ge(p_ot, n + 1)
                    if n >= 1:
                        dve.wait_ge(p_y, n)
                    V.tensor_copy(oT[:, :, :].rearrange("p h (b t) -> p b h t", b=BT),
                                  tail[:, 0:256].rearrange("p (b h t) -> p b h t", b=BT, h=2)).then_inc(v_ot, 1)

                def s_x3():
                    dve.wait_ge(p_y, n + 1)
                    V.tensor_tensor(xs[:, n, :], tail[:, 0:256], xs[:, n, :], ALU.add).then_inc(v_x3, 1)

                def s_x3t():
                    dve.wait_ge(p_x3t, n + 1)
                    V.tensor_copy(x3T[:, :, :], tail[:, 0:256].rearrange("p (c t) -> p c t", c=2)).then_inc(v_x3t, 1)

                def s_xam():
                    dve.wait_ge(p_xa, n + 1)
                    V.tensor_tensor(xam[:, :].rearrange("p (b t) -> p b t", b=BT),
                                    tail[:, 256:384].rearrange("p (b t) -> p b t", b=BT),
                                    amask[:, BT * n:BT * n + BT].unsqueeze(2).broadcast_to([128, BT, T]),
                                    ALU.mult).then_inc(v_xam, 1)

                def s_fin():
                    dve.wait_ge(p_h, n + 1)
                    V.tensor_tensor(xs[:, n, :], tail[:, 0:256], xs[:, n, :], ALU.add).then_inc(v_fin, 1)

                return [s_norm, s_ot, s_x3, s_x3t, s_xam, s_fin]

            def tail_work(i):
                k = i - (BT + 2)
                n, r = k // BT, k % BT
                if 0 <= n < NT:
                    st = steps(n)
                    if r == 0:
                        st[0]()
                        st[1]()
                    if r == 1:
                        st[2]()
                    if r == 2:
                        st[3]()
                    if r == 3:
                        st[4]()
                        st[5]()

            for i in range(B + BT + 3):
                if i < B:
                    dve.wait_ge(p_s, i + 1)
                    link(V.tensor_reduce(nmax[:, i, :], bank[S_BANK[i % 3]][:, 0:2 * NKEY]
                                         .rearrange("p (g c) -> p g c", g=2), AX.X, ALU.max))
                    V.tensor_scalar(nmax[:, i, :], nmax[:, i, :], -SCALE, None, ALU.mult).then_inc(v_max, 1)
                if i < B and i % 2 == 0:
                    dve.wait_ge(p_v2, i // 2 + 1)
                    if i >= 4:
                        dve.wait_ge(p_o, i - 2)
                    V.tensor_copy(V2[0:HK, i % 4:i % 4 + 2, :],
                                  bank[V2_BANK][0:HK, :].rearrange("p (b n) -> p b n", b=2)).then_inc(v_v2, 1)
                tail_work(i)

        @block.tensor
        def _(pe):
            M = nc.tensor.matmul
            X = nc.tensor.transpose
            pe.wait_ge(s_cb, 16)

            def weights(k, parts):
                if k >= 2:
                    pe.wait_ge(a_wt, k - 1)
                for q, src in enumerate(parts):
                    last = X(bank[WT_BANK[k % 2]][:, 128 * q:128 * q + 128], src, ident)
                last.then_inc(p_wt, 1)

            def half(w, c, h):
                return w[:, h, 128 * c:128 * c + 128]

            pe.wait_ge(v_hot, 1)
            pe.wait_ge(s_small, 16 * (3 + NA))
            M(bank[2][:, 0:B], fside_sb[:, :, :].rearrange("s a d -> s (a d)"), hot[:, :], start=True, stop=True)\
                .then_inc(p_bias, 1)
            pe.wait_ge(s_wqkv, 48)
            weights(0, [half(wq_sb, c, h) for c in range(2) for h in range(2)])
            weights(1, [half(wkv_sb, c, h) for c in range(2) for h in range(2)])
            for m, (banks, done, added) in enumerate(((L0_BANK, p_l0, v_x1), (L1_BANK, p_l1, v_x2))):
                pe.wait_ge(v_bd, m + 1)
                for g in range(4):
                    if m == 0:
                        pe.wait_ge(s_x[g // 2], 16)
                        if g >= 2:
                            pe.wait_ge(v_x1, 2 * (g - 1))
                    else:
                        pe.wait_ge(v_x1, 2 * (g + 1))
                        if g >= 2:
                            pe.wait_ge(v_x2, g - 1)
                    for n in (2 * g, 2 * g + 1):
                        last = M(bank[banks[g % 2]][:, 256 * (n % 2):256 * (n % 2) + 256], bd[:, m, n, :],
                                 xs[:, n, :], start=True, stop=True)
                    last.then_inc(done, 1)
            pe.wait_ge(v_perm, NT)
            for n in range(NT):
                pe.wait_ge(v_x2, n // 2 + 1)
                if n >= 2:
                    pe.wait_ge(a_xt, n - 1)
                    pe.wait_ge(v_xto, n - 1)
                else:
                    pe.wait_ge(v_x1, NT)
                for c in range(2):
                    X(bank[XT_BANK[n % 2]][:, 128 * c:128 * c + 128], half(xs, c, n), ident)
                for c in range(2):
                    last = M(bank[XTO_BANK[n % 2]][:, 128 * c:128 * c + 128], half(xs, c, n),
                             perm[:, n, :], start=True, stop=True, is_transpose=True)
                last.then_inc(p_xt, 1)
            pe.wait_ge(s_w3, 64)
            weights(2, [half(w3_sb, c, h) for c in range(2) for h in range(2)])
            weights(3, [a3_sb[:, 0:128], a3_sb[:, 128:256]]
                    + [b3_sb[:, h, :, :].rearrange("p a r -> p (a r)") for h in range(2)])
            pe.wait_ge(s_wo, 64)
            weights(4, [wo_sb[:, o, h, :] for h in range(2) for o in range(2)])
            pe.wait_ge(v_diag, RT)
            pe.wait_ge(g_ones, 1)
            pe.wait_ge(a_wt, 5)
            pe.wait_ge(v_xto, NT)
            for h in range(2):
                M(bank[h][:, :], ones[:, :], diag_w[:, 4 * h:4 * h + 4, :], start=True, stop=True)
            for j in range(RT):
                last = M(bank[3][:, BR * NSLOT * j:BR * NSLOT * j + RP[j]], ones[0:RP[j], :],
                         diag_r[0:RP[j], j, 0:RP[j]], start=True, stop=True)
            last.then_inc(p_idx, 1)

            def queries(n):
                pe.wait_ge(v_rope, 2 * n + 1)
                if n >= 2:
                    pe.wait_ge(a_qt, n - 1)
                for h in range(2):
                    last = X(bank[QT_BANK[n % 2]][:, 128 * h:128 * h + 128],
                             qr[:, n % 2, 128 * h:128 * h + 128], ident)
                last.then_inc(p_qt, 1)

            pe.wait_ge(a_xt, NT)
            pe.wait_ge(a_wrow, 2)
            for n in range(NT):
                if n >= 3:
                    pe.wait_ge(a_z, 2 * (n - 2))
                z = bank[Z_BANK[n % 3]]
                for c in range(2):
                    M(z[:, 0:256], xT[:, c, 128 * n:128 * n + 128], wqkvT[:, c, 0:256], start=(c == 0), stop=(c == 1))
                for c in range(2):
                    last = M(z[:, 256:512], xTo[:, c, 2 * n:2 * n + 2, :, :].rearrange("p o b i -> p (o b i)"),
                             wqkvT[:, c, 256:512], start=(c == 0), stop=(c == 1))
                last.then_inc(p_z, 1)
                if n >= 2:
                    queries(n - 2)
            queries(NT - 2)
            queries(NT - 1)
            for k in range(NT1):
                kind, o = k // BLK, k % BLK
                clean = (kz, vz)[kind]
                z = bank[T1_BANK[k % 6]]
                if k == 0:
                    pe.wait_ge(a_wrow, 3)
                    pe.wait_ge(a_z, 2 * NT)
                    pe.wait_ge(v_rope, 2 * NT)
                    pe.wait_ge(v_oh, 8)
                if o == 0:
                    pe.wait_ge((g_zk, g_zv)[kind], RT)
                if k >= 6:
                    pe.wait_ge((v_t1, a_t1)[k % 2], (k - 6) // 2 + 1)
                for j in range(RT):
                    M(z[:, BR * NSLOT * j:BR * NSLOT * j + RP[j]],
                      clean[0:RP[j], j, 128 * o:128 * o + 128], ident[0:RP[j], 0:RP[j]],
                      start=(j == 0), stop=False, is_transpose=True, skip_group_check=True)
                w = slice(64 * (o % 2), 64 * (o % 2) + 64)
                M(z[:, 0:NR], new[w, o // 2, kind, :], OH[w, o // 2, :], start=False, stop=True,
                  skip_group_check=True).then_inc(p_t1, 1)

            tail = bank[TAIL_BANK]

            def scores(b):
                if b >= 3:
                    pe.wait_ge(a_exp, 2 * (b - 2))
                n = b // BT
                if b % BT == 0:
                    pe.wait_ge(g_qb, G * (n + 1))
                z = bank[S_BANK[b % 3]][:, 0:2 * NKEY].rearrange("p (g c) -> p g c", g=2)
                M(z, spread[:, b % BT, :], maskb[:, n, :].unsqueeze(1).broadcast_to([128, 2, NKEY]),
                  start=True, stop=False)
                for g in range(2):
                    last = M(z[:, g, :], QB[:, n % NQB, b % BT, g, :], KT[:, b, :], start=False, stop=(g == 1))
                last.then_inc(p_s, 1)

            def values(b):
                if b >= 2:
                    pe.wait_ge(v_v2, b // 2)
                for q in range(4):
                    last = X(bank[V2_BANK][0:HK, 128 * q:128 * q + 128],
                             VT[:, b + q // 2, HK * (q % 2):HK * (q % 2) + HK], ident)
                last.then_inc(p_v2, 1)

            def turn_probs(b):
                pe.wait_ge(a_exp, 2 * (b + 1))
                if b >= 2:
                    pe.wait_ge(a_pt, b - 1)
                for g in range(2):
                    for c in range(2):
                        q = 2 * g + c
                        last = X(bank[PT_BANK[b % 2]][0:HK, 128 * q:128 * q + 128],
                                 P[:, b % 3, g, HK * c:HK * c + HK], ident)
                last.then_inc(p_pt, 1)

            def weigh(b):
                pe.wait_ge(a_pt, b + 1)
                pe.wait_ge(v_v2, b // 2 + 1)
                if b % BT == 0 and b >= BT:
                    pe.wait_ge(v_osb, 2 * (b // BT))
                for g in range(2):
                    z = bank[O_BANK][:, 128 * (b % BT) + 64 * g:128 * (b % BT) + 64 * g + 64]
                    for c in range(2):
                        q = 2 * g + c
                        last = M(z, PT[0:HK, b % 2, 128 * q:128 * q + 128],
                                 V2[0:HK, b % 4, 128 * c + 64 * g:128 * c + 64 * g + 64],
                                 start=(c == 0), stop=(c == 1))
                last.then_inc(p_o, 1)

            def heads(n):
                pe.wait_ge(v_osb, 2 * (n + 1))
                if n >= 1:
                    pe.wait_ge(v_fin, n)
                for b in range(BT):
                    last = M(tail[:, 64 * b:64 * b + 64], osb[:, b, :, :, :].rearrange("p k g d -> p (k g d)"),
                             B_("merge"), start=True, stop=True)
                last.then_inc(p_ot, 1)

            def project(n):
                pe.wait_ge(v_ot, n + 1)
                for h in range(2):
                    last = M(tail[:, 0:256], oT[:, h, :], woT[:, h, :], start=(h == 0), stop=(h == 1))
                last.then_inc(p_y, 1)

            def turn_x3(n):
                pe.wait_ge(v_x3, n + 1)
                for c in range(2):
                    last = X(tail[:, 128 * c:128 * c + 128], half(xs, c, n), ident)
                last.then_inc(p_x3t, 1)

            def adapter_in(n):
                pe.wait_ge(v_x3t, n + 1)
                for c in range(2):
                    last = M(tail[:, 256:384], abT[:, 128 * c:128 * c + 128], x3T[:, c, :],
                             start=(c == 0), stop=(c == 1))
                last.then_inc(p_xa, 1)

            def adapter_out(n):
                pe.wait_ge(v_xam, n + 1)
                for c in range(2):
                    M(tail[:, 0:256], x3T[:, c, :], w3T[:, c, :], start=(c == 0), stop=False)
                M(tail[:, 0:256], xam[:, :], abT[:, 256:512], start=False, stop=True).then_inc(p_h, 1)

            pe.wait_ge(v_mask, 1)
            pe.wait_ge(a_same, BT)
            pe.wait_ge(v_t1, NT1 // 2)
            pe.wait_ge(a_t1, NT1 // 2)
            for i in range(B + BT + 3):
                n, r = (i - BT - 2) // BT, (i - BT - 2) % BT
                on = 0 <= n < NT
                if i < B:
                    scores(i)
                    if i % 2 == 0:
                        values(i)
                if on and r == 1:
                    project(n)
                if on and r == 3:
                    adapter_in(n)
                if 2 <= i < B + 2:
                    turn_probs(i - 2)
                if 3 <= i < B + 3:
                    weigh(i - 3)
                if on and r == 0:
                    heads(n)
                if on and r == 2:
                    turn_x3(n)
                if on and r == 3:
                    adapter_out(n)


_INS = ['x', 'itok_B_0_7', 'fside_8xS_0', 'itok_B_1_198', 'itok_Bx257_0_4111', 'itok_B_37_3939', 'itok_B_0_6',
        'L0_cond_weights', 'L1_cond_weights', 'L2_cond_Wq', 'L2_cond_Wk', 'L2_cond_Wv', 'L2_cond_Wo',
        'L2_cond_q_norm_scale', 'L2_cond_k_norm_scale', 'L2_cond_k_blocks', 'L2_cond_v_blocks', 'L3_cond_W',
        'L3_cond_A', 'L3_cond_Bm', 'L3_cond_scalings']


def kernel(**inputs):
    import numpy as _np
    import concourse.bacc as _bacc
    from concourse import mybir as _mybir
    from concourse.bass_utils import run_bass_kernel_spmd as _run

    nc = _bacc.Bacc("TRN2", target_bir_lowering=False, num_devices=1)
    arrays, args = {}, []

    def give(name, a):
        arrays[name] = a
        args.append(nc.dram_tensor(name, a.shape, _mybir.dt.from_np(a.dtype), kind="ExternalInput").ap())

    for name in _INS:
        give(f"in_{name}_dram", _np.ascontiguousarray(inputs[name]))
    for name, a in zip(("const_a", "const_b"), constants()):
        give(name, a)
    args.append(nc.dram_tensor("out_0_dram", (B, T, D), _mybir.dt.float32, kind="ExternalOutput").ap())
    build(nc, *args)
    r = _run(nc, [arrays], core_ids=[0])
    return r.results[0]["out_0_dram"]
```

```python
import concourse.bass as bass
from concourse import mybir
from contextlib import ExitStack
import numpy as np

B, T, D = 32, 32, 256
TOK = B * T
NT = TOK // 128
BT = 128 // T
S0, S1 = 8, 200
H, G, HD = 8, 4, 32
BLK, WIN, NBLK = 16, 128, 257
NPOOL = 16 * NBLK
NSLOT = (WIN - 1 + T + BLK - 2) // BLK + 1
NKEY = NSLOT * BLK
HK = NKEY // 2
BR = 128 // NSLOT
RT = (B + BR - 1) // BR
RP = [min(BR, B - j * BR) * NSLOT for j in range(RT)]
NR = B * NSLOT
NA, RANK = 8, 16
SCALE = 256.0 ** -0.5
EPS = 1e-6
BIG = float(2.0 ** 100)
MAGIC = 1.5 * 2.0 ** 23
TWO_PI_HI = 6.28125
TWO_PI_LO = float(2 * np.pi - 6.28125)
PI_SAFE = 3.1415925

COLS_A = [("batch_in_tile", BT), ("channel", 1), ("read_batch", RT * B), ("slot", RT), ("read_row", RT),
          ("write_batch", B), ("half", 1), ("write_row", 1), ("offset", 8), ("code", 1), ("adapter", 1),
          ("index", 1), ("group_parity", 2), ("inv_freq", 16), ("half_sign", 32), ("subject", 2), ("same_channel", 32)]
COLS_B = [("ident", 128), ("iota", 128), ("later", 128), ("distance", NKEY), ("same_token", 128)]


def columns(table):
    at, out = 0, {}
    for name, n in table:
        out[name] = (at, at + n)
        at += n
    return out, at


AT_A, WA = columns(COLS_A)
AT_B, WB = columns(COLS_B)


def constants():
    p = np.arange(128)
    v = {}
    v["batch_in_tile"] = (p[:, None] // T == np.arange(BT)[None]).astype(np.float32)
    v["channel"] = (p % 32)[:, None]
    rb = np.arange(RT)[None] * BR + p[:, None] // NSLOT
    v["read_batch"] = (rb[:, :, None] == np.arange(B)[None, None]).reshape(128, -1)
    v["slot"] = np.repeat((p % NSLOT)[:, None], RT, 1)
    v["read_row"] = rb * NBLK
    wb = (p % 64) // 2
    v["write_batch"] = wb[:, None] == np.arange(B)[None]
    v["half"] = (p % 2)[:, None]
    v["write_row"] = (wb * NBLK)[:, None]
    v["offset"] = 2 * np.arange(8)[None] + (p // 64)[:, None]
    v["code"] = ((p // T) * 2 + (p % T) // 16)[:, None]
    v["adapter"] = (p // RANK)[:, None]
    v["index"] = p[:, None]
    v["group_parity"] = ((p // 32) % 2)[:, None] == np.arange(2)[None]
    inv = 1.0 / np.float32(10000.0) ** (np.arange(16, dtype=np.float32) / np.float32(16))
    v["inv_freq"] = np.repeat(inv[None].astype(np.float32), 128, 0)
    v["half_sign"] = np.repeat(np.where(np.arange(32) < 16, 1.0, -1.0)[None], 128, 0)
    v["subject"] = p[:, None] // 32 + 4 * np.arange(2)[None]
    v["same_channel"] = (p[:, None] % 32) == np.arange(32)[None]
    v["ident"] = p[:, None] == p[None]
    v["iota"] = np.repeat(p[None], 128, 0)
    v["later"] = (p[None] > p[:, None]) & (p[None] // 64 == p[:, None] // 64)
    c = np.arange(NKEY)
    v["distance"] = (c % NSLOT * BLK + c // NSLOT)[None] - (p % T)[:, None]
    v["same_token"] = (p[:, None] % T) == (p[None] % T)
    a = np.concatenate([v[n].astype(np.float32) for n, _ in COLS_A], 1)
    b = np.concatenate([v[n].astype(np.float32) for n, _ in COLS_B], 1)
    return np.ascontiguousarray(a), np.ascontiguousarray(b)


def build(nc, x, index_rows, fside, table, w0, w1, wqkvT_in, woT_in, norm_scales, kblocks, vblocks, w3T_in,
          aT_in, bT_in, scaling_rows, const_a, const_b, out):
    f32, bf16, i32 = mybir.dt.float32, mybir.dt.bfloat16, mybir.dt.int32
    ALU, ACT, AX = mybir.AluOpType, mybir.ActivationFunctionType, mybir.AxisListType

    x_rows = x.rearrange("(n b) t d -> (b t) n d", b=BT)
    out_rows = out.rearrange("(n b) t d -> (b t) n d", b=BT)
    table_rows = table.rearrange("b (n o) -> (b n) o", o=1)
    w1_rows = w1.rearrange("s c d -> (s c) d")
    k_rows = kblocks.rearrange("n g o d -> n (g o d)")
    v_rows = vblocks.rearrange("n g o d -> n (g o d)")

    ctx = ExitStack()
    with ctx:
        def sb(name, shape, dt=f32):
            return ctx.enter_context(nc.sbuf_tensor(name, shape, dt))

        def sem(name):
            return ctx.enter_context(nc.semaphore(name))

        NZ = 4
        ca = sb("ca", [128, WA])
        cb = sb("cb", [128, WB])

        def A_(name):
            return ca[:, AT_A[name][0]:AT_A[name][1]]

        def B_(name):
            return cb[:, AT_B[name][0]:AT_B[name][1]]

        ident = B_("ident")
        ones = sb("ones", [128, 128])
        spread = sb("spread", [128, BT, 128], bf16)
        vec_i = sb("vec_i", [128, 4, B], i32)
        vec = sb("vec", [128, 4, B])
        pick4 = sb("pick4", [128, 4, NT, BT])
        tokv = sb("tokv", [128, 4, NT])
        idx1f = sb("idx1f", [128, NT])
        idx1 = sb("idx1", [128, NT], i32)
        rtmp = sb("rtmp", [128, RT, B])
        rkv = sb("rkv", [128, 4, RT])
        ridx = sb("ridx", [128, RT], i32)
        rblk_i = sb("rblk_i", [128, RT], i32)
        rblk = sb("rblk", [128, RT])
        wtmp = sb("wtmp", [128, B])
        wkv = sb("wkv", [128, 8])
        widx = sb("widx", [128, 2], i32)
        wtab_i = sb("wtab_i", [128, 2], i32)
        wtab = sb("wtab", [128, 4])
        wrap = sb("wrap", [128, 8])
        wblk = sb("wblk", [128, 8])
        wlive = sb("wlive", [128, 8])
        dead = sb("dead", [128, 8])
        hot = sb("hot", [S0, B])
        bias_all = sb("bias_all", [128, NT, BT])
        bias = sb("bias", [128, NT])
        tok = sb("tok", [128, 6, NT])
        pos = sb("pos", [128, 2 * NT])
        trig = sb("trig", [128, 2, 2 * NT, 16])
        nscale = sb("nscale", [128, 2, HD])
        nsign = sb("nsign", [128, 2, HD])
        rope_c = sb("rope_c", [128, 2 * NT, HD])
        rope_s = sb("rope_s", [128, 2 * NT, HD])
        dist = sb("dist", [128, 2, NKEY])
        maskb = sb("maskb", [128, NT, NKEY], bf16)
        fside_sb = sb("fside_sb", [S0, BT, HD])
        scal = sb("scal", [128, 1])
        amask = sb("amask", [128, B])
        w0_sb = sb("w0_sb", [128, 2, 32])
        subj = sb("subj", [128, 2, B])
        wg = sb("wg", [128, NT, 32])
        xs = sb("xs", [128, NT, D])
        kz = sb("kz", [128, RT, BLK * 128])
        early = kz[:, :, :].rearrange("p j n -> p (j n)")
        bd = early[:, 0:2048].rearrange("p (m n q) -> p m n q", m=2, n=NT)
        ang = early[:, 4608:4864].rearrange("p (n i) -> p n i", n=2 * NT)
        turn = early[:, 4864:5376].rearrange("p (k n i) -> p k n i", k=2, n=2 * NT)
        red = early[:, 5376:5888].rearrange("p (k n i) -> p k n i", k=2, n=2 * NT)
        wqkvT = sb("wqkvT", [128, 2, 512])
        w3T = sb("w3T", [128, 2, D])
        abT = sb("abT", [128, 512])
        woT = sb("woT", [128, 2, D])
        zs = sb("zs", [128, NZ, 384])
        sq = sb("sq", [128, 2, 384])
        ra = sb("ra", [128, 12, HD])
        rb = sb("rb", [128, 12, HD])
        ss = sb("ss", [128, 2, 4, 12])
        qr = sb("qr", [128, NT, D])
        new = sb("new", [128, 8, 2, 128])
        QT = sb("QT", [128, B, 2 * T])
        kraw = sb("kraw", [128, RT, BLK * 128])
        vraw = sb("vraw", [128, RT, BLK * 128])
        keep = sb("keep", [128, RT, BLK])
        OH = sb("OH", [128, 8, NR])
        KT = sb("KT", [128, B, NKEY])
        VT = sb("VT", [128, B, NKEY])
        kt = KT[:, :, :].rearrange("p b c -> p (b c)")
        xT = kt[:, 0:2048].rearrange("p (c t) -> p c t", c=2)
        xTo = kt[:, 2048:4096].rearrange("p (c o b i) -> p c o b i", c=2, o=BLK, b=B)
        perm = kt[:, 4096:5120].rearrange("p (n q) -> p n q", n=NT)
        vflat = VT[:, :, :].rearrange("p b c -> p (b c)")
        diag_w = vflat[:, 0:1024].rearrange("p (j q) -> p j q", j=8)
        wrow = vflat[:, 1024:2048]
        eq = vflat[:, 2048:3072]
        diag_r = vflat[:, 3072:3456].rearrange("p (j q) -> p j q", j=3)
        rrow = vflat[:, 3456:3456 + NR]
        pick0 = vflat[:, 3584:5632].rearrange("p (k n) -> p k n", k=2)
        vz = kraw
        NQB = 4
        QB = early[:, 0:NQB * 1024].rearrange("p (k b g q) -> p k b g q", k=NQB, b=BT, g=2)
        kflat = vraw[:, :, :].rearrange("p j n -> p (j n)")

        def carve(at, n):
            return kflat[:, at:at + n], at + n

        P_, at = carve(0, 3 * 2 * NKEY)
        P = P_.rearrange("p (k g c) -> p k g c", k=3, g=2)
        PT_, at = carve(at, 2 * 512)
        PT = PT_.rearrange("p (k n) -> p k n", k=2)
        V2_, at = carve(at, 4 * 256)
        V2 = V2_.rearrange("p (k n) -> p k n", k=4)
        oT = sb("oT", [128, 2, 128])
        x3T = sb("x3T", [128, 2, 128])
        xam = sb("xam", [128, 128])
        nmax = sb("nmax", [128, B, 2])
        rsum = sb("rsum", [128, B, 2])
        rinv = sb("rinv", [128, B, 2])

        bank = [ctx.enter_context(nc.psum_tensor(f"bank{i}", [128, 512], f32)) for i in range(8)]

        s_vec = sem("s_vec")
        s_ca = sem("s_ca")
        s_cb = sem("s_cb")
        s_x = [sem("s_x0"), sem("s_x1")]
        s_w0 = sem("s_w0")
        s_small = sem("s_small")
        s_wqkv = sem("s_wqkv")
        s_w3 = sem("s_w3")
        s_g1 = sem("s_g1")
        s_rt = sem("s_rt")
        s_wt = sem("s_wt")
        s_k = sem("s_k")
        s_v = sem("s_v")
        s_out = sem("s_out")

        v_idx1 = sem("v_idx1")
        v_pick0 = sem("v_pick0")
        v_idxt = sem("v_idxt")
        v_ridx = sem("v_ridx")
        v_hot = sem("v_hot")
        v_perm = sem("v_perm")
        v_bd = sem("v_bd")
        v_angles = sem("v_angles")
        v_mask = sem("v_mask")
        v_diag = sem("v_diag")
        v_oh = sem("v_oh")
        v_keep = sem("v_keep")
        v_x1 = sem("v_x1")
        v_x2 = sem("v_x2")
        v_zread = sem("v_zread")
        v_sqread = sem("v_sqread")
        v_ms = sem("v_ms")
        v_mid = sem("v_mid")
        v_dist = sem("v_dist")
        v_rope = sem("v_rope")
        v_max = sem("v_max")
        v_v2 = sem("v_v2")
        v_norm = sem("v_norm")
        v_x3 = sem("v_x3")
        v_xam = sem("v_xam")
        v_fin = sem("v_fin")
        v_chain = sem("v_chain")

        g_ones = sem("g_ones")
        g_zk = sem("g_zk")
        g_zv = sem("g_zv")
        g_qb = sem("g_qb")

        a_ot = sem("a_ot")
        a_x3t = sem("a_x3t")
        a_same = sem("a_same")
        a_trig = sem("a_trig")
        a_wrow = sem("a_wrow")
        a_xt = sem("a_xt")
        a_sq = sem("a_sq")
        a_root = sem("a_root")
        a_z = sem("a_z")
        a_dist = sem("a_dist")
        a_qt = sem("a_qt")
        a_t1 = sem("a_t1")
        a_exp = sem("a_exp")
        a_pt = sem("a_pt")

        p_pick = sem("p_pick")
        p_bias = sem("p_bias")
        p_l0 = sem("p_l0")
        p_l1 = sem("p_l1")
        p_xt = sem("p_xt")
        p_idx = sem("p_idx")
        p_z = sem("p_z")
        p_qt = sem("p_qt")
        p_t1 = sem("p_t1")
        p_s = sem("p_s")
        p_v2 = sem("p_v2")
        p_pt = sem("p_pt")
        p_o = sem("p_o")
        p_y = sem("p_y")
        p_x3t = sem("p_x3t")
        p_xa = sem("p_xa")
        p_h = sem("p_h")

        PICK_BANK = [0, 1]
        L0_BANK = [3, 4]
        L1_BANK = [5, 6]
        XT_BANK = [7, 2]
        Z_BANK = [4, 5, 6]
        QT_BANK = [0, 1]
        T1_BANK = [2, 3, 7, 4, 5, 6]
        S_BANK = [0, 1, 2]
        PT_BANK = [3, 4]
        V2_BANK, O_BANK, TAIL_BANK = 5, 6, 7
        NT1 = 2 * BLK

        def t1_dst(k):
            return (KT if k < BLK else VT)[:, :, NSLOT * (k % BLK):NSLOT * (k % BLK) + NSLOT]

        def t1_src(k):
            return bank[T1_BANK[k % 6]][:, 0:NR].rearrange("p (b s) -> p b s", b=B)

        block = ctx.enter_context(nc.Block())

        @block.sync
        def _(sp):
            sp.dma_start(vec_i[:, :, :], index_rows.partition_broadcast(128)).then_inc(s_vec, 16)
            sp.dma_start(ca[:, :], const_a).then_inc(s_ca, 16)
            sp.dma_start(w0_sb[:, :, :], w0.rearrange("(k s) c d -> (s c) k d", k=2)).then_inc(s_w0, 16)
            sp.dma_start(fside_sb[:, :, :], fside.rearrange("s (a d) -> s a d", a=1).broadcast_to([S0, BT, HD]))\
                .then_inc(s_w0, 16)
            sp.dma_start(xs[:, 0:4, :], x_rows[:, 0:4, :]).then_inc(s_x[0], 16)
            sp.dma_start(xs[:, 4:8, :], x_rows[:, 4:8, :]).then_inc(s_x[1], 16)
            sp.dma_start(cb[:, :], const_b).then_inc(s_cb, 16)
            sp.dma_start(wqkvT[:, :, :], wqkvT_in).then_inc(s_wqkv, 16)
            sp.dma_start(nscale[:, :, :], norm_scales.partition_broadcast(128)).then_inc(s_small, 16)
            sp.dma_start(scal[:, :], scaling_rows).then_inc(s_small, 16)
            sp.dma_start(woT[:, :, :], woT_in).then_inc(s_w3, 16)
            sp.dma_start(w3T[:, :, :], w3T_in).then_inc(s_w3, 16)
            sp.dma_start(abT[:, 0:256].rearrange("p (c n) -> p c n", c=2), aT_in).then_inc(s_w3, 16)
            sp.dma_start(abT[:, 256:512], bT_in).then_inc(s_w3, 16)
            for n in range(NT):
                sp.wait_ge(v_fin, n + 1)
                sp.dma_start(out_rows[:, n, :], xs[:, n, :]).then_inc(s_out, 16)
            sp.wait_ge(s_out, 16 * NT)

        @block.gpsimd
        def _(pool):
            pool.memset(ones[:, :], 1.0).then_inc(g_ones, 1)

            def gather(dst, src, idx, done):
                pool.indirect_dma_start(out=dst, out_offset=None, in_=src,
                                        in_offset=bass.IndirectOffsetOnAxis(ap=idx, axis=0)).then_inc(done, 16)

            pool.wait_ge(v_idx1, 1)
            for n in range(NT):
                gather(wg[:, n, :], w1_rows, idx1[:, n:n + 1], s_g1)
            pool.wait_ge(v_idxt, 1)
            for j in range(RT):
                gather(rblk_i[0:RP[j], j:j + 1], table_rows, ridx[0:RP[j], j:j + 1], s_rt)
            for j in range(2):
                gather(wtab_i[:, j:j + 1], table_rows, widx[:, j:j + 1], s_wt)
            pool.wait_ge(s_rt, 16 * RT)
            for j in range(RT):
                gather(kraw[0:RP[j], j, :], k_rows, rblk_i[0:RP[j], j:j + 1], s_k)
            for j in range(RT):
                gather(vraw[0:RP[j], j, :], v_rows, rblk_i[0:RP[j], j:j + 1], s_v)
            pool.wait_ge(v_keep, 1)
            for raw, dst, landed, done in ((kraw, kz, s_k, g_zk), (vraw, vz, s_v, g_zv)):
                pool.wait_ge(landed, 16 * RT)
                for j in range(RT):
                    if dst is vz:
                        pool.wait_ge(g_zk, j + 1)
                    pool.tensor_tensor(dst[0:RP[j], j, :].rearrange("p (o g d) -> p g o d", g=G, o=BLK),
                                       raw[0:RP[j], j, :].rearrange("p (g o d) -> p g o d", g=G, o=BLK),
                                       keep[0:RP[j], j, :].unsqueeze(1).unsqueeze(3)
                                       .broadcast_to([RP[j], G, BLK, HD]), ALU.mult).then_inc(done, 1)

            pool.wait_ge(p_t1, BLK)
            pool.wait_ge(a_qt, NT)
            for n in range(NT):
                if n >= NQB:
                    pool.wait_ge(p_s, BT * (n - NQB + 1))
                for g in range(G):
                    src = QT[:, BT * n:BT * n + BT, :]
                    pool.tensor_tensor(QB[:, n % NQB, :, g // 2, 64 * (g % 2):64 * (g % 2) + 64], src,
                                       A_("batch_in_tile")[:, g:g + 1].unsqueeze(2).broadcast_to([128, BT, 2 * T]),
                                       ALU.mult).then_inc(g_qb, 1)

        @block.scalar
        def _(act):
            act.wait_ge(s_ca, 16)
            act.wait_ge(s_cb, 16)
            for b in range(BT):
                nc.scalar.activation(spread[:, b, :], B_("same_token"), ACT.Copy,
                                     scale=A_("batch_in_tile")[:, b:b + 1]).then_inc(a_same, 1)
            act.wait_ge(v_angles, 1)
            nc.scalar.activation(trig[:, :, :, :], red[:, :, :, :], ACT.Sin).then_inc(a_trig, 1)
            for n in range(NT):
                act.wait_ge(p_xt, n + 1)
                nc.scalar.activation(xT[:, :, 128 * n:128 * n + 128],
                                     bank[XT_BANK[n % 2]][:, 0:256].rearrange("p (c t) -> p c t", c=2),
                                     ACT.Copy).then_inc(a_xt, 1)
                nc.scalar.activation(xTo[:, :, :, BT * n:BT * n + BT, :].rearrange("p c o b i -> p c o (b i)"),
                                     bank[XT_BANK[n % 2]][:, 256:512].rearrange("p (c o e) -> p c o e", c=2, o=BLK),
                                     ACT.Copy).then_inc(a_xt, 1)
            act.wait_ge(p_idx, 1)
            for h in range(2):
                nc.scalar.activation(wrow[:, 512 * h:512 * h + 512], bank[h][:, :], ACT.Copy).then_inc(a_wrow, 1)
            nc.scalar.activation(rrow, bank[3][:, 0:NR], ACT.Copy).then_inc(a_wrow, 1)

            def queries_out(n):
                act.wait_ge(p_qt, n + 1)
                src = bank[QT_BANK[n % 2]][:, 0:256].rearrange("p (h b t) -> p b h t", h=2, b=BT)
                dst = QT[:, BT * n:BT * n + BT, :].rearrange("p b (h t) -> p b h t", h=2)
                nc.scalar.activation(dst, src, ACT.Copy).then_inc(a_qt, 1)

            def root(n):
                act.wait_ge(v_ms, n + 1)
                nc.scalar.activation(ss[:, n % 2, 2, :], ss[:, n % 2, 1, :], ACT.Sqrt).then_inc(a_root, 1)

            for n in range(NT):
                act.wait_ge(p_z, n + 1)
                z = bank[Z_BANK[n % 3]]
                if n >= NZ:
                    act.wait_ge(v_zread, n - NZ + 1)
                nc.scalar.activation(zs[:, n % NZ, :], z[:, 0:384], ACT.Copy).then_inc(a_z, 1)
                nc.scalar.activation(new[:, n, 1, :], z[:, 384:512], ACT.Copy).then_inc(a_z, 1)
                act.wait_ge(a_z, 2 * n + 1)
                if n >= 2:
                    act.wait_ge(v_sqread, n - 1)
                nc.scalar.activation(sq[:, n % 2, :], zs[:, n % NZ, :], ACT.Square).then_inc(a_sq, 1)
                if n >= 1:
                    root(n - 1)
            root(NT - 1)
            for k in range(NT1):
                if k < BLK and k % 2 == 0:
                    queries_out(k // 2)
                act.wait_ge(p_t1, k + 1)
                nc.scalar.activation(t1_dst(k), t1_src(k), ACT.Copy).then_inc(a_t1, 1)
                if k >= BLK and k % 2 == 0:
                    n = (k - BLK) // 2
                    act.wait_ge(v_mid, 1)
                    if n >= 2:
                        act.wait_ge(v_dist, n - 1)
                    nc.scalar.activation(dist[:, n % 2, :], B_("distance"), ACT.Square, bias=tok[:, 5, n:n + 1])\
                        .then_inc(a_dist, 1)

            def pt_out(b):
                act.wait_ge(p_pt, b + 1)
                if b >= 2:
                    act.wait_ge(p_o, b - 1)
                nc.scalar.activation(PT[0:HK, b % 2, :], bank[PT_BANK[b % 2]][0:HK, :], ACT.Copy).then_inc(a_pt, 1)

            def heads_out(n):
                act.wait_ge(p_o, BT * n + BT)
                if n >= 1:
                    act.wait_ge(p_y, n)
                nc.scalar.activation(oT[:, :, :].rearrange("p h (b t) -> p b h t", b=BT),
                                     bank[O_BANK][:, 0:256].rearrange("p (b h t) -> p b h t", b=BT, h=2),
                                     ACT.Copy).then_inc(a_ot, 1)

            def x3_out(n):
                act.wait_ge(p_x3t, n + 1)
                nc.scalar.activation(x3T[:, :, :], bank[TAIL_BANK][:, 0:256].rearrange("p (c t) -> p c t", c=2),
                                     ACT.Copy).then_inc(a_x3t, 1)

            for i in range(B + 6):
                if i < B:
                    act.wait_ge(v_max, i + 1)
                    if i >= 3:
                        act.wait_ge(p_pt, i - 2)
                    for g in range(2):
                        nc.scalar.activation(P[:, i % 3, g, :], bank[S_BANK[i % 3]][:, NKEY * g:NKEY * g + NKEY],
                                             ACT.Exp, bias=nmax[:, i, g:g + 1], scale=SCALE,
                                             accum_out=rsum[:, i, g:g + 1]).then_inc(a_exp, 1)
                if 2 <= i < B + 2:
                    pt_out(i - 2)
                if i >= 6 and (i - 6) % BT == 0:
                    heads_out((i - 6) // BT)
                if i >= 8 and (i - 8) % BT == 0:
                    x3_out((i - 8) // BT)

        @block.vector
        def _(dve):
            V = nc.vector
            chain = [0]

            def link(ins):
                chain[0] += 1
                ins.then_inc(v_chain, 1)
                dve.wait_ge(v_chain, chain[0])

            def blocks_of(dst, src):
                link(V.tensor_scalar(dst, src, (1.0 - BLK) / 2, 1.0 / BLK, ALU.add, ALU.mult))
                link(V.tensor_scalar(dst, dst, MAGIC, None, ALU.add))
                link(V.tensor_scalar(dst, dst, MAGIC, None, ALU.subtract))

            dve.wait_ge(s_vec, 16)
            dve.wait_ge(s_ca, 16)
            link(V.tensor_copy(vec[:, :, :], vec_i[:, :, :]))
            link(V.tensor_tensor(pick4[:, :, :, :], vec[:, :, :].rearrange("p v (n b) -> p v n b", b=BT),
                                 A_("batch_in_tile").unsqueeze(1).unsqueeze(1).broadcast_to([128, 4, NT, BT]),
                                 ALU.mult))
            link(V.tensor_reduce(tokv[:, :, :], pick4[:, :, :, :], AX.X, ALU.add))
            link(V.tensor_scalar(idx1f[:, :], tokv[:, 1, :], 32.0, A_("channel"), ALU.mult, ALU.add))
            V.tensor_copy(idx1[:, :], idx1f[:, :]).then_inc(v_idx1, 1)
            for k in range(2):
                picked = V.tensor_scalar(subj[:, k, :], vec[:, 0, :], A_("subject")[:, k:k + 1], None, ALU.is_equal)
            link(picked)
            for h in range(2):
                b = slice(B // 2 * h, B // 2 * h + B // 2)
                V.tensor_tensor(pick0[:, :, 512 * h:512 * h + 512].rearrange("p k (b c) -> p k b c", c=32),
                                subj[:, :, b].unsqueeze(3).broadcast_to([128, 2, B // 2, 32]),
                                A_("same_channel").unsqueeze(1).unsqueeze(1).broadcast_to([128, 2, B // 2, 32]),
                                ALU.mult).then_inc(v_pick0, 1)
            V.tensor_scalar(hot[:, :], vec[0:S0, 0, :], A_("index")[0:S0, :], None, ALU.is_equal).then_inc(v_hot, 1)
            link(V.tensor_tensor(rtmp[:, :, :], A_("read_batch").rearrange("p (j b) -> p j b", j=RT),
                                 vec[:, 2, :].unsqueeze(1).broadcast_to([128, RT, B]), ALU.mult))
            link(V.tensor_reduce(rkv[:, 0, :], rtmp[:, :, :], AX.X, ALU.add))
            link(V.tensor_scalar(rkv[:, 1, :], rkv[:, 0, :], float(1 - WIN), 0.0, ALU.add, ALU.max))
            blocks_of(rkv[:, 2, :], rkv[:, 1, :])
            link(V.tensor_tensor(rkv[:, 0, :], rkv[:, 2, :], A_("slot"), ALU.add))
            V.tensor_tensor(ridx[:, :], rkv[:, 0, :], A_("read_row"), ALU.add)
            link(V.tensor_tensor(wtmp[:, :], A_("write_batch"), vec[:, 2, :], ALU.mult))
            link(V.tensor_reduce(wkv[:, 0:1], wtmp[:, :], AX.X, ALU.add))
            blocks_of(wkv[:, 2:3], wkv[:, 0:1])
            link(V.scalar_tensor_tensor(wkv[:, 1:2], wkv[:, 2:3], float(-BLK), wkv[:, 0:1], ALU.mult, ALU.add))
            link(V.tensor_tensor(wkv[:, 3:4], wkv[:, 2:3], A_("half"), ALU.add))
            link(V.tensor_tensor(wkv[:, 4:5], wkv[:, 3:4], A_("write_row"), ALU.add))
            V.tensor_copy(widx[:, 0:1], wkv[:, 4:5])
            V.tensor_scalar(widx[:, 1:2], wkv[:, 4:5], 1.0, None, ALU.add).then_inc(v_idxt, 1)
            link(V.tensor_scalar(tok[:, 0, :], tokv[:, 2, :], A_("channel"), None, ALU.add))
            blocks_of(tok[:, 2, :], tok[:, 0, :])
            link(V.scalar_tensor_tensor(tok[:, 1, :], tok[:, 2, :], float(-BLK), tok[:, 0, :], ALU.mult, ALU.add))
            link(V.tensor_scalar(tok[:, 2, :], tok[:, 1, :], 8.0, A_("code"), ALU.mult, ALU.add))
            dve.wait_ge(s_cb, 16)
            for n in range(NT):
                V.tensor_scalar(perm[:, n, :], B_("iota"), tok[:, 2, n:n + 1], None, ALU.is_equal).then_inc(v_perm, 1)

            def block_diagonal(m, h, src):
                n = slice(4 * h, 4 * h + 4)
                V.tensor_tensor(bd[:, m, n, :].rearrange("p n (b d) -> p n b d", b=BT),
                                src.unsqueeze(2).broadcast_to([128, 4, BT, 32]),
                                A_("batch_in_tile").unsqueeze(1).unsqueeze(3).broadcast_to([128, 4, BT, 32]),
                                ALU.mult).then_inc(v_bd, 1)

            for h in range(2):
                dve.wait_ge(p_pick, h + 1)
                block_diagonal(0, h, bank[PICK_BANK[h]][:, 0:128].rearrange("p (n d) -> p n d", n=4))
            dve.wait_ge(p_bias, 1)
            link(V.tensor_tensor(bias_all[:, :, :], bank[2][:, 0:B].rearrange("p (n b) -> p n b", b=BT),
                                 A_("batch_in_tile").unsqueeze(1).broadcast_to([128, NT, BT]), ALU.mult))
            link(V.tensor_reduce(bias[:, :], bias_all[:, :, :], AX.X, ALU.add))
            for g in range(4):
                dve.wait_ge(p_l0, g + 1)
                for n in (2 * g, 2 * g + 1):
                    V.scalar_tensor_tensor(xs[:, n, :], bank[L0_BANK[g % 2]][:, 256 * (n % 2):256 * (n % 2) + 256],
                                           bias[:, n:n + 1], xs[:, n, :], ALU.add, ALU.add).then_inc(v_x1, 1)
            V.tensor_scalar(wrap[:, :], A_("offset"), wkv[:, 1:2], None, ALU.is_lt)
            V.tensor_copy(pos[:, 0:NT], tok[:, 0, :])
            link(V.tensor_scalar(wkv[:, 5:6], wkv[:, 3:4], float(BLK), None, ALU.mult))
            link(V.scalar_tensor_tensor(pos[:, NT:2 * NT], wrap[:, :], float(BLK), A_("offset"), ALU.mult, ALU.add))
            link(V.tensor_scalar(pos[:, NT:2 * NT], pos[:, NT:2 * NT], wkv[:, 5:6], None, ALU.add))
            link(V.tensor_tensor(ang[:, :, :], pos[:, :].unsqueeze(2).broadcast_to([128, 2 * NT, 16]),
                                 A_("inv_freq").unsqueeze(1).broadcast_to([128, 2 * NT, 16]), ALU.mult))
            for k in range(2):
                link(V.tensor_scalar(turn[:, k, :, :], ang[:, :, :], float(1 / (2 * np.pi)), 0.25 * k,
                                     ALU.mult, ALU.add))
            link(V.tensor_scalar(turn[:, :, :, :], turn[:, :, :, :], MAGIC, None, ALU.add))
            link(V.tensor_scalar(turn[:, :, :, :], turn[:, :, :, :], MAGIC, None, ALU.subtract))
            for k in range(2):
                link(V.scalar_tensor_tensor(red[:, k, :, :], turn[:, k, :, :], -TWO_PI_HI, ang[:, :, :],
                                            ALU.mult, ALU.add))
            link(V.scalar_tensor_tensor(red[:, :, :, :], turn[:, :, :, :], -TWO_PI_LO, red[:, :, :, :],
                                        ALU.mult, ALU.add))
            link(V.tensor_scalar(red[:, 1, :, :], red[:, 1, :, :], float(np.pi / 2), None, ALU.add))
            V.tensor_scalar(red[:, :, :, :], red[:, :, :, :], PI_SAFE, -PI_SAFE, ALU.min, ALU.max)\
                .then_inc(v_angles, 1)
            dve.wait_ge(s_g1, 16 * NT)
            for h in range(2):
                block_diagonal(1, h, wg[:, 4 * h:4 * h + 4, :])
            for g in range(4):
                dve.wait_ge(p_l1, g + 1)
                V.tensor_tensor(xs[:, 2 * g:2 * g + 2, :],
                                bank[L1_BANK[g % 2]][:, :].rearrange("p (n d) -> p n d", n=2),
                                xs[:, 2 * g:2 * g + 2, :], ALU.add).then_inc(v_x2, 1)
            dve.wait_ge(s_small, 32)
            dve.wait_ge(a_trig, 1)
            link(V.tensor_scalar(nscale[:, :, :], nscale[:, :, :], 1.0, float(HD) ** 0.5, ALU.add, ALU.mult))
            link(V.tensor_tensor(nsign[:, :, :], nscale[:, :, :],
                                 A_("half_sign").unsqueeze(1).broadcast_to([128, 2, HD]), ALU.mult))
            for k in range(2):
                t = slice(NT * k, NT * k + NT)
                for f, (dst, sc) in enumerate(((rope_s, nsign), (rope_c, nscale))):
                    last = V.tensor_tensor(
                        dst[:, t, :].rearrange("p n (h i) -> p n h i", h=2),
                        trig[:, f, t, :].unsqueeze(2).broadcast_to([128, NT, 2, 16]),
                        sc[:, k, :].rearrange("p (h i) -> p h i", h=2).unsqueeze(1).broadcast_to([128, NT, 2, 16]),
                        ALU.mult)
            link(last)

            dve.wait_ge(s_wt, 32)
            dve.wait_ge(s_rt, 16 * RT)
            link(V.tensor_copy(wtab[:, 0:2], wtab_i[:, :]))
            link(V.tensor_tensor(wtab[:, 2:3], wtab[:, 1:2], wtab[:, 0:1], ALU.subtract))
            link(V.tensor_scalar(wblk[:, :], wrap[:, :], wtab[:, 2:3], wtab[:, 0:1], ALU.mult, ALU.add))
            V.tensor_tensor(diag_w, ident.unsqueeze(1).broadcast_to([128, 8, 128]),
                            wblk[:, :].unsqueeze(2).broadcast_to([128, 8, 128]), ALU.mult)
            for j in range(RT):
                link(V.tensor_copy(rblk[0:RP[j], j:j + 1], rblk_i[0:RP[j], j:j + 1]))
                V.tensor_scalar(diag_r[0:RP[j], j, 0:RP[j]], ident[0:RP[j], 0:RP[j]], rblk[0:RP[j], j:j + 1], None,
                                ALU.mult).then_inc(v_diag, 1)
            dve.wait_ge(a_wrow, 3)
            eq3 = eq.rearrange("p (j q) -> p j q", j=8)
            link(V.tensor_tensor(eq3, wrow.rearrange("p (j q) -> p j q", j=8),
                                 wblk[:, :].unsqueeze(2).broadcast_to([128, 8, 128]), ALU.is_equal))
            link(V.tensor_tensor(eq3, eq3, B_("later").unsqueeze(1).broadcast_to([128, 8, 128]), ALU.mult))
            link(V.tensor_reduce(dead[:, :], eq3, AX.X, ALU.max))
            link(V.scalar_tensor_tensor(wlive[:, :], dead[:, :], -10000.0, wblk[:, :], ALU.mult, ALU.add))
            for j in range(8):
                V.tensor_scalar(OH[:, j, :], rrow, wlive[:, j:j + 1], None, ALU.is_equal).then_inc(v_oh, 1)
            for j in range(RT):
                link(V.tensor_scalar(eq[0:RP[j], :], wrow[0:RP[j], :], rblk[0:RP[j], j:j + 1], None, ALU.is_equal))
                link(V.tensor_reduce(keep[0:RP[j], j, :], eq[0:RP[j], :].rearrange("p (o q) -> p o q", o=BLK), AX.X,
                                     ALU.max))
                kept = V.tensor_scalar(keep[0:RP[j], j, :], keep[0:RP[j], j, :], -1.0, 1.0, ALU.mult, ALU.add)
                if j < RT - 1:
                    link(kept)
            kept.then_inc(v_keep, 1)
            for n in range(NT):
                dve.wait_ge(a_z, 2 * n + 1)
                if n >= 1:
                    dve.wait_ge(v_rope, 2 * n)
                zq = zs[:, n % NZ, 0:256].rearrange("p (h d) -> p h d", h=H)
                zk = zs[:, n % NZ, 256:384].rearrange("p (h d) -> p h d", h=G)
                V.tensor_tensor(ra[:, 0:H, :], zq, rope_c[:, n, :].unsqueeze(1).broadcast_to([128, H, HD]), ALU.mult)
                V.tensor_tensor(ra[:, H:12, :], zk, rope_c[:, NT + n, :].unsqueeze(1).broadcast_to([128, G, HD]),
                                ALU.mult)
                V.tensor_tensor(rb[:, 0:H, :], zq, rope_s[:, n, :].unsqueeze(1).broadcast_to([128, H, HD]), ALU.mult)
                V.tensor_tensor(rb[:, H:12, :], zk, rope_s[:, NT + n, :].unsqueeze(1).broadcast_to([128, G, HD]),
                                ALU.mult).then_inc(v_zread, 1)
                dve.wait_ge(v_zread, n + 1)
                dve.wait_ge(a_sq, n + 1)
                V.tensor_reduce(ss[:, n % 2, 0, :], sq[:, n % 2, :].rearrange("p (h d) -> p h d", h=12), AX.X,
                                ALU.add).then_inc(v_sqread, 1)
                dve.wait_ge(v_sqread, n + 1)
                V.tensor_scalar(ss[:, n % 2, 1, :], ss[:, n % 2, 0, :], HD * EPS, None, ALU.add).then_inc(v_ms, 1)
                link(V.tensor_tensor(ra[:, :, :].rearrange("p h (k i) -> p h k i", k=2),
                                     ra[:, :, :].rearrange("p h (k i) -> p h k i", k=2),
                                     rb[:, :, :].rearrange("p h (k i) -> p h k i", k=2)[:, :, ::-1, :], ALU.add))
                dve.wait_ge(a_root, n + 1)
                link(V.reciprocal(ss[:, n % 2, 3, :], ss[:, n % 2, 2, :]))
                V.tensor_tensor(qr[:, n, :].rearrange("p (h g d) -> p g h d", h=2, g=G),
                                ra[:, 0:H, :].rearrange("p (g h) d -> p g h d", h=2),
                                ss[:, n % 2, 3, 0:H].rearrange("p (g h) -> p g h", h=2).unsqueeze(3)
                                .broadcast_to([128, G, 2, HD]), ALU.mult).then_inc(v_rope, 1)
                V.tensor_tensor(new[:, n, 0, :].rearrange("p (h d) -> p h d", h=G), ra[:, H:12, :],
                                ss[:, n % 2, 3, H:12].unsqueeze(2).broadcast_to([128, G, HD]), ALU.mult).then_inc(v_rope, 1)
            link(V.tensor_scalar(tok[:, 1, :], tokv[:, 2, :], float(1 - WIN), 0.0, ALU.add, ALU.max))
            blocks_of(tok[:, 3, :], tok[:, 1, :])
            link(V.scalar_tensor_tensor(tok[:, 4, :], tok[:, 3, :], float(BLK), tokv[:, 2, :], ALU.mult, ALU.subtract))
            V.tensor_scalar(tok[:, 5, :], tok[:, 4, :], WIN / 2 - 0.5, None, ALU.add).then_inc(v_mid, 1)
            for n in range(NT):
                dve.wait_ge(a_dist, n + 1)
                V.tensor_scalar(maskb[:, n, :], dist[:, n % 2, :], (WIN / 2) ** 2, -BIG, ALU.is_gt, ALU.mult)\
                    .then_inc(v_dist, 1)
            V.tensor_scalar(amask[:, :], vec[:, 3, :], A_("adapter"), scal[:, 0:1], ALU.is_equal, ALU.mult)\
                .then_inc(v_mask, 1)
            tail = bank[TAIL_BANK]

            def normalise(b):
                dve.wait_ge(a_exp, 2 * (b + 1))
                link(V.reciprocal(rinv[:, b, :], rsum[:, b, :]))
                for g in range(2):
                    V.tensor_scalar(P[:, b % 3, g, :], P[:, b % 3, g, :], rinv[:, b, g:g + 1], None, ALU.mult)\
                        .then_inc(v_norm, 1)

            def add_attention(n):
                dve.wait_ge(p_y, n + 1)
                V.tensor_tensor(xs[:, n, :], tail[:, 0:256], xs[:, n, :], ALU.add).then_inc(v_x3, 1)

            def pick_adapter(n):
                dve.wait_ge(p_xa, n + 1)
                V.tensor_tensor(xam[:, :].rearrange("p (b t) -> p b t", b=BT),
                                tail[:, 256:384].rearrange("p (b t) -> p b t", b=BT),
                                amask[:, BT * n:BT * n + BT].unsqueeze(2).broadcast_to([128, BT, T]),
                                ALU.mult).then_inc(v_xam, 1)

            def add_last(n):
                dve.wait_ge(p_h, n + 1)
                V.tensor_tensor(xs[:, n, :], tail[:, 0:256], xs[:, n, :], ALU.add).then_inc(v_fin, 1)

            for i in range(B + 7):
                if i < B:
                    dve.wait_ge(p_s, i + 1)
                    link(V.tensor_reduce(nmax[:, i, :], bank[S_BANK[i % 3]][:, 0:2 * NKEY]
                                         .rearrange("p (g c) -> p g c", g=2), AX.X, ALU.max))
                    V.tensor_scalar(nmax[:, i, :], nmax[:, i, :], -SCALE, None, ALU.mult).then_inc(v_max, 1)
                if 1 <= i < B + 1:
                    normalise(i - 1)
                if i < B and i % 2 == 0:
                    dve.wait_ge(p_v2, i // 2 + 1)
                    if i >= 4:
                        dve.wait_ge(p_o, i - 2)
                    V.tensor_copy(V2[0:HK, i % 4:i % 4 + 2, :],
                                  bank[V2_BANK][0:HK, :].rearrange("p (b n) -> p b n", b=2)).then_inc(v_v2, 1)
                n, r = (i - 7) // BT, (i - 7) % BT
                if n >= 0:
                    if r == 0:
                        add_attention(n)
                    if r == 2:
                        pick_adapter(n)
                    if r == 3:
                        add_last(n)

        @block.tensor
        def _(pe):
            M = nc.tensor.matmul
            X = nc.tensor.transpose

            def half(w, c, h):
                return w[:, h, 128 * c:128 * c + 128]

            pe.wait_ge(s_w0, 32)
            for h in range(2):
                pe.wait_ge(v_pick0, h + 1)
                for n in range(4):
                    for k in range(2):
                        last = M(bank[PICK_BANK[h]][:, 32 * n:32 * n + 32],
                                 pick0[:, k, 512 * h + 128 * n:512 * h + 128 * n + 128], w0_sb[:, k, :],
                                 start=(k == 0), stop=(k == 1))
                last.then_inc(p_pick, 1)
            pe.wait_ge(v_hot, 1)
            M(bank[2][:, 0:B], fside_sb[:, :, :].rearrange("s a d -> s (a d)"), hot[:, :], start=True, stop=True)\
                .then_inc(p_bias, 1)
            for m, (banks, done, added) in enumerate(((L0_BANK, p_l0, v_x1), (L1_BANK, p_l1, v_x2))):
                for g in range(4):
                    pe.wait_ge(v_bd, 2 * m + g // 2 + 1)
                    if m == 0:
                        pe.wait_ge(s_x[g // 2], 16)
                        if g >= 2:
                            pe.wait_ge(v_x1, 2 * (g - 1))
                    else:
                        pe.wait_ge(v_x1, 2 * (g + 1))
                        if g >= 2:
                            pe.wait_ge(v_x2, g - 1)
                    for n in (2 * g, 2 * g + 1):
                        last = M(bank[banks[g % 2]][:, 256 * (n % 2):256 * (n % 2) + 256], bd[:, m, n, :],
                                 xs[:, n, :], start=True, stop=True)
                    last.then_inc(done, 1)
            pe.wait_ge(s_cb, 16)
            pe.wait_ge(v_perm, NT)
            for n in range(NT):
                pe.wait_ge(v_x2, n // 2 + 1)
                if n >= 2:
                    pe.wait_ge(a_xt, 2 * (n - 1))
                else:
                    pe.wait_ge(v_x1, NT)
                for c in range(2):
                    X(bank[XT_BANK[n % 2]][:, 128 * c:128 * c + 128], half(xs, c, n), ident)
                for c in range(2):
                    last = M(bank[XT_BANK[n % 2]][:, 256 + 128 * c:384 + 128 * c], half(xs, c, n),
                             perm[:, n, :], start=True, stop=True, is_transpose=True)
                last.then_inc(p_xt, 1)
            pe.wait_ge(v_diag, RT)
            pe.wait_ge(g_ones, 1)
            pe.wait_ge(v_bd, 2)
            for h in range(2):
                M(bank[h][:, :], ones[:, :], diag_w[:, 4 * h:4 * h + 4, :], start=True, stop=True)
            for j in range(RT):
                last = M(bank[3][:, BR * NSLOT * j:BR * NSLOT * j + RP[j]], ones[0:RP[j], :],
                         diag_r[0:RP[j], j, 0:RP[j]], start=True, stop=True)
            last.then_inc(p_idx, 1)

            def queries(n):
                pe.wait_ge(v_rope, 2 * n + 1)
                if n >= 2:
                    pe.wait_ge(a_qt, n - 1)
                for h in range(2):
                    last = X(bank[QT_BANK[n % 2]][:, 128 * h:128 * h + 128],
                             qr[:, n, 128 * h:128 * h + 128], ident)
                last.then_inc(p_qt, 1)

            pe.wait_ge(s_wqkv, 16)
            pe.wait_ge(a_xt, 2 * NT)
            pe.wait_ge(a_wrow, 2)
            for n in range(NT):
                if n >= 3:
                    pe.wait_ge(a_z, 2 * (n - 2))
                z = bank[Z_BANK[n % 3]]
                for c in range(2):
                    M(z[:, 0:256], xT[:, c, 128 * n:128 * n + 128], wqkvT[:, c, 0:256], start=(c == 0), stop=(c == 1))
                for c in range(2):
                    last = M(z[:, 256:512], xTo[:, c, 2 * n:2 * n + 2, :, :].rearrange("p o b i -> p (o b i)"),
                             wqkvT[:, c, 256:512], start=(c == 0), stop=(c == 1))
                last.then_inc(p_z, 1)
            for k in range(NT1):
                kind, o = k // BLK, k % BLK
                clean = (kz, vz)[kind]
                z = bank[T1_BANK[k % 6]]
                if k == 0:
                    pe.wait_ge(a_wrow, 3)
                    pe.wait_ge(a_z, 2 * NT)
                if kind == 0 and o % 2 == 0:
                    queries(o // 2)
                    pe.wait_ge(v_rope, 2 * (o // 2) + 2)
                    pe.wait_ge(v_oh, o // 2 + 1)
                if o == 0:
                    pe.wait_ge((g_zk, g_zv)[kind], RT)
                if k >= 6:
                    pe.wait_ge(a_t1, k - 5)
                for j in range(RT):
                    M(z[:, BR * NSLOT * j:BR * NSLOT * j + RP[j]],
                      clean[0:RP[j], j, 128 * o:128 * o + 128], ident[0:RP[j], 0:RP[j]],
                      start=(j == 0), stop=False, is_transpose=True, skip_group_check=True)
                w = slice(64 * (o % 2), 64 * (o % 2) + 64)
                M(z[:, 0:NR], new[w, o // 2, kind, :], OH[w, o // 2, :], start=False, stop=True,
                  skip_group_check=True).then_inc(p_t1, 1)

            tail = bank[TAIL_BANK]

            def scores(b):
                if b >= 3:
                    pe.wait_ge(a_exp, 2 * (b - 2))
                n = b // BT
                if b % BT == 0:
                    pe.wait_ge(g_qb, G * (n + 1))
                z = bank[S_BANK[b % 3]][:, 0:2 * NKEY].rearrange("p (g c) -> p g c", g=2)
                M(z, spread[:, b % BT, :], maskb[:, n, :].unsqueeze(1).broadcast_to([128, 2, NKEY]),
                  start=True, stop=False)
                for g in range(2):
                    last = M(z[:, g, :], QB[:, n % NQB, b % BT, g, :], KT[:, b, :], start=False, stop=(g == 1))
                last.then_inc(p_s, 1)

            def values(b):
                if b >= 2:
                    pe.wait_ge(v_v2, b // 2)
                for q in range(4):
                    last = X(bank[V2_BANK][0:HK, 128 * q:128 * q + 128],
                             VT[:, b + q // 2, HK * (q % 2):HK * (q % 2) + HK], ident)
                last.then_inc(p_v2, 1)

            def turn_probs(b):
                pe.wait_ge(v_norm, 2 * (b + 1))
                if b >= 2:
                    pe.wait_ge(a_pt, b - 1)
                for g in range(2):
                    for c in range(2):
                        q = 2 * g + c
                        last = X(bank[PT_BANK[b % 2]][0:HK, 128 * q:128 * q + 128],
                                 P[:, b % 3, g, HK * c:HK * c + HK], ident)
                last.then_inc(p_pt, 1)

            def weigh(b):
                pe.wait_ge(a_pt, b + 1)
                pe.wait_ge(v_v2, b // 2 + 1)
                if b % BT == 0 and b >= BT:
                    pe.wait_ge(a_ot, b // BT)
                for c in range(2):
                    for g in range(G):
                        last = M(bank[O_BANK][32 * g:32 * g + 32, 64 * (b % BT):64 * (b % BT) + 64],
                                 V2[0:HK, b % 4, 128 * c + 32 * g:128 * c + 32 * g + 32],
                                 PT[0:HK, b % 2, 128 * (2 * (g // 2) + c) + 64 * (g % 2):
                                    128 * (2 * (g // 2) + c) + 64 * (g % 2) + 64],
                                 start=(c == 0), stop=(c == 1))
                last.then_inc(p_o, 1)

            def project(n):
                pe.wait_ge(a_ot, n + 1)
                if n >= 1:
                    pe.wait_ge(v_fin, n)
                for h in range(2):
                    last = M(tail[:, 0:256], oT[:, h, :], woT[:, h, :], start=(h == 0), stop=(h == 1))
                last.then_inc(p_y, 1)

            def turn_x3(n):
                pe.wait_ge(v_x3, n + 1)
                for c in range(2):
                    last = X(tail[:, 128 * c:128 * c + 128], half(xs, c, n), ident)
                last.then_inc(p_x3t, 1)

            def adapter_in(n):
                pe.wait_ge(a_x3t, n + 1)
                for c in range(2):
                    last = M(tail[:, 256:384], abT[:, 128 * c:128 * c + 128], x3T[:, c, :],
                             start=(c == 0), stop=(c == 1))
                last.then_inc(p_xa, 1)

            def adapter_out(n):
                pe.wait_ge(v_xam, n + 1)
                for c in range(2):
                    M(tail[:, 0:256], x3T[:, c, :], w3T[:, c, :], start=(c == 0), stop=False)
                M(tail[:, 0:256], xam[:, :], abT[:, 256:512], start=False, stop=True).then_inc(p_h, 1)

            pe.wait_ge(v_mask, 1)
            pe.wait_ge(a_same, BT)
            pe.wait_ge(a_t1, NT1)
            pe.wait_ge(a_qt, NT)
            pe.wait_ge(s_w3, 64)
            for i in range(B + 7):
                n, r = (i - 7) // BT, (i - 7) % BT
                if i < B:
                    scores(i)
                    if i % 2 == 0:
                        values(i)
                if n >= 0 and r == 2:
                    adapter_in(n)
                if n >= 0 and r == 3:
                    adapter_out(n)
                if 2 <= i < B + 2:
                    turn_probs(i - 2)
                if n >= 0 and r == 0:
                    project(n)
                if n >= 0 and r == 1:
                    turn_x3(n)
                if 3 <= i < B + 3:
                    weigh(i - 3)



def kernel(**inputs):
    import numpy as _np
    import concourse.bacc as _bacc
    from concourse import mybir as _mybir
    from concourse.bass_utils import run_bass_kernel_spmd as _run

    nc = _bacc.Bacc("TRN2", target_bir_lowering=False, num_devices=1)
    arrays, args = {}, []

    def give(name, a):
        a = _np.ascontiguousarray(a)
        name = "in_" + name
        arrays[name] = a
        args.append(nc.dram_tensor(name, a.shape, _mybir.dt.from_np(a.dtype), kind="ExternalInput").ap())

    def rows(w):
        return w.T.reshape(2, 128, w.shape[0]).transpose(1, 0, 2)

    i = inputs
    give("x", i["x"])
    give("index_rows", _np.stack([i["itok_B_0_7"], i["itok_B_1_198"], i["itok_B_37_3939"], i["itok_B_0_6"]]))
    give("fside", i["fside_8xS_0"])
    give("block_table", i["itok_Bx257_0_4111"])
    give("mix0_weights", i["L0_cond_weights"])
    give("mix1_weights", i["L1_cond_weights"])
    give("wqkvT", rows(_np.concatenate([i["L2_cond_Wq"], i["L2_cond_Wk"], i["L2_cond_Wv"]], 0)))
    give("woT", i["L2_cond_Wo"].reshape(D, G, 2, HD).transpose(1, 3, 2, 0).reshape(128, 2, D))
    give("norm_scales", _np.stack([i["L2_cond_q_norm_scale"], i["L2_cond_k_norm_scale"]]))
    give("k_blocks", i["L2_cond_k_blocks"])
    give("v_blocks", i["L2_cond_v_blocks"])
    give("w3T", rows(i["L3_cond_W"]))
    give("aT", rows(i["L3_cond_A"].reshape(NA * RANK, D)))
    give("bT", i["L3_cond_Bm"].transpose(0, 2, 1).reshape(NA * RANK, D))
    give("scaling_rows", _np.repeat(i["L3_cond_scalings"], RANK)[:, None])
    for name, a in zip(("const_a", "const_b"), constants()):
        give(name, a)
    args.append(nc.dram_tensor("out_0_dram", (B, T, D), _mybir.dt.float32, kind="ExternalOutput").ap())
    build(nc, *args)
    r = _run(nc, [arrays], core_ids=[0])
    return r.results[0]["out_0_dram"]
```

```python
import concourse.bass as bass
from concourse import mybir
from contextlib import ExitStack
import numpy as np

B, T, D = 32, 32, 256
TOK = B * T
NT = TOK // 128
BT = 128 // T
S0, S1 = 8, 200
H, G, HD = 8, 4, 32
BLK, WIN, NBLK = 16, 128, 257
NPOOL = 16 * NBLK
NSLOT = (WIN - 1 + T + BLK - 2) // BLK + 1
NKEY = NSLOT * BLK
HK = NKEY // 2
BR = 128 // NSLOT
RT = (B + BR - 1) // BR
RP = [min(BR, B - j * BR) * NSLOT for j in range(RT)]
NR = B * NSLOT
NA, RANK = 8, 16
SCALE = 256.0 ** -0.5
EPS = 1e-6
BIG = float(2.0 ** 100)
MAGIC = 1.5 * 2.0 ** 23
TWO_PI_HI = 6.28125
TWO_PI_LO = float(2 * np.pi - 6.28125)
PI_SAFE = 3.1415925

COLS_A = [("batch_in_tile", BT), ("channel", 1), ("read_batch", RT * B), ("slot", RT), ("read_row", RT),
          ("write_batch", B), ("half", 1), ("write_row", 1), ("offset", 8), ("code", 1), ("adapter", 1),
          ("index", 1), ("inv_freq", 16), ("half_sign", 32), ("subject", 2), ("same_channel", 32), ("other_parity", 2)]
COLS_B = [("ident", 128), ("iota", 128), ("later", 128), ("distance", NKEY)]


def columns(table):
    at, out = 0, {}
    for name, n in table:
        out[name] = (at, at + n)
        at += n
    return out, at


AT_A, WA = columns(COLS_A)
AT_B, WB = columns(COLS_B)


def constants():
    p = np.arange(128)
    v = {}
    v["batch_in_tile"] = (p[:, None] // T == np.arange(BT)[None]).astype(np.float32)
    v["channel"] = (p % 32)[:, None]
    rb = np.arange(RT)[None] * BR + p[:, None] // NSLOT
    v["read_batch"] = (rb[:, :, None] == np.arange(B)[None, None]).reshape(128, -1)
    v["slot"] = np.repeat((p % NSLOT)[:, None], RT, 1)
    v["read_row"] = rb * NBLK
    wb = (p % 64) // 2
    v["write_batch"] = wb[:, None] == np.arange(B)[None]
    v["half"] = (p % 2)[:, None]
    v["write_row"] = (wb * NBLK)[:, None]
    v["offset"] = 2 * np.arange(8)[None] + (p // 64)[:, None]
    v["code"] = ((p // T) * 2 + (p % T) // 16)[:, None]
    v["adapter"] = (p // RANK)[:, None]
    v["index"] = p[:, None]
    inv = 1.0 / np.float32(10000.0) ** (np.arange(16, dtype=np.float32) / np.float32(16))
    v["inv_freq"] = np.repeat(inv[None].astype(np.float32), 128, 0)
    v["half_sign"] = np.repeat(np.where(np.arange(32) < 16, 1.0, -1.0)[None], 128, 0)
    v["subject"] = p[:, None] // 32 + 4 * np.arange(2)[None]
    v["same_channel"] = (p[:, None] % 32) == np.arange(32)[None]
    v["other_parity"] = np.where((p // 64)[:, None] == np.arange(2)[None], 0.0, -100000.0)
    v["ident"] = p[:, None] == p[None]
    v["iota"] = np.repeat(p[None], 128, 0)
    v["later"] = (p[None] > p[:, None]) & (p[None] // 64 == p[:, None] // 64)
    c = np.arange(NKEY)
    v["distance"] = (c % NSLOT * BLK + c // NSLOT)[None] - (p % T)[:, None]
    a = np.concatenate([v[n].astype(np.float32) for n, _ in COLS_A], 1)
    b = np.concatenate([v[n].astype(np.float32) for n, _ in COLS_B], 1)
    return np.ascontiguousarray(a), np.ascontiguousarray(b)


def build(nc, x, index_rows, fside, table, w0, w1, wqkvT_in, woT_in, norm_scales, kblocks, vblocks, w3T_in,
          aT_in, bT_in, scaling_rows, const_a, const_b, out):
    f32, bf16, i32 = mybir.dt.float32, mybir.dt.bfloat16, mybir.dt.int32
    ALU, ACT, AX = mybir.AluOpType, mybir.ActivationFunctionType, mybir.AxisListType

    x_rows = x.rearrange("(n b) t d -> (b t) n d", b=BT)
    out_rows = out.rearrange("(n b) t d -> (b t) n d", b=BT)
    table_rows = table.rearrange("b (n o) -> (b n) o", o=1)
    w1_rows = w1.rearrange("s c d -> (s c) d")
    k_rows = kblocks.rearrange("n g o d -> n (g o d)")
    v_rows = vblocks.rearrange("n g o d -> n (g o d)")

    ctx = ExitStack()
    with ctx:
        def sb(name, shape, dt=f32):
            return ctx.enter_context(nc.sbuf_tensor(name, shape, dt))

        def sem(name):
            return ctx.enter_context(nc.semaphore(name))

        ca = sb("ca", [128, WA])
        cb = sb("cb", [128, WB])

        def A_(name):
            return ca[:, AT_A[name][0]:AT_A[name][1]]

        def B_(name):
            return cb[:, AT_B[name][0]:AT_B[name][1]]

        ident = B_("ident")
        vec_i = sb("vec_i", [128, 4, B], i32)
        vec = sb("vec", [128, 4, B])
        tokv = sb("tokv", [128, 4, NT])
        idx1f = sb("idx1f", [128, NT])
        idx1 = sb("idx1", [128, NT], i32)
        rkv = sb("rkv", [128, 4, RT])
        ridx = sb("ridx", [128, RT], i32)
        rblk_i = sb("rblk_i", [128, RT], i32)
        rblk = sb("rblk", [128, RT])
        wtmp = sb("wtmp", [128, B])
        wkv = sb("wkv", [128, 8])
        widx = sb("widx", [128, 2], i32)
        wtab_i = sb("wtab_i", [128, 2], i32)
        wtab = sb("wtab", [128, 4])
        wrap = sb("wrap", [128, 8])
        wblk = sb("wblk", [128, 8])
        wlive = sb("wlive", [128, 8])
        dead = sb("dead", [128, 8])
        hot = sb("hot", [S0, B])
        bias_all = sb("bias_all", [128, NT, BT])
        bias = sb("bias", [128, NT])
        tok = sb("tok", [128, 6, NT])
        pos = sb("pos", [128, 2 * NT])
        trig = sb("trig", [128, 2, 2 * NT, 16])
        nscale = sb("nscale", [128, 2, HD])
        nsign = sb("nsign", [128, 2, HD])
        rope_c = sb("rope_c", [128, 2 * NT, HD])
        rope_s = sb("rope_s", [128, 2 * NT, HD])
        dist = sb("dist", [128, 2, NKEY])
        mid = sb("mid", [128, 4, B])
        kept = dist[0:BLK, :, :].rearrange("p k c -> p (k c)")
        fside_sb = sb("fside_sb", [S0, BT, HD])
        scal = sb("scal", [128, 1])
        amask = sb("amask", [128, B])
        w0_sb = sb("w0_sb", [128, 2, 32])
        subj = sb("subj", [128, 2, B])
        wg = sb("wg", [128, NT, 32])
        xs = sb("xs", [128, NT, D])
        kz = sb("kz", [128, RT, BLK * 128])
        early = kz[:, :, :].rearrange("p j n -> p (j n)")
        bd = early[:, 0:2048].rearrange("p (m n q) -> p m n q", m=2, n=NT)
        wqkvT = sb("wqkvT", [128, 2, 512])
        w3T = sb("w3T", [128, 2, D])
        abT = sb("abT", [128, 512])
        sq_a = sb("sq_a", [128, NT // 2, 384])
        ra = sb("ra", [128, 2, 12, HD])
        rb = sb("rb", [128, 2, 12, HD])
        ss = sb("ss", [128, 3, NT, 12])
        eps = sb("eps", [128, 1])
        strip = sb("strip", [128, 2 * BLK - 1], bf16)
        wlive16 = sb("wlive16", [128, BLK])
        qr = sb("qr", [128, NT, D])
        new = sb("new", [128, 8, 2, 128])
        kraw = sb("kraw", [128, RT, BLK * 128])
        vraw = sb("vraw", [128, RT, BLK * 128])
        keep = sb("keep", [128, RT, BLK])
        parts = sb("parts", [128, 3, NT, 2, 128], bf16)
        OH = sb("OH", [128, BLK, NR], bf16)
        KT = sb("KT", [128, B, NKEY])
        VT = sb("VT", [128, B, NKEY])
        kt = KT[:, :, :].rearrange("p b c -> p (b c)")
        xT = kt[:, 0:2048].rearrange("p (c t) -> p c t", c=2)
        xTo = kt[:, 2048:4096].rearrange("p (c o b i) -> p c o b i", c=2, o=BLK, b=B)
        perm = kt[:, 4096:5120].rearrange("p (n q) -> p n q", n=NT)
        sq_b = kt[:, 4096:4096 + NT // 2 * 384].rearrange("p (n q) -> p n q", n=NT // 2)

        def squares(n, count):
            return (sq_a, sq_b)[n // (NT // 2)][:, n % (NT // 2):n % (NT // 2) + count, :]

        vflat = VT[:, :, :].rearrange("p b c -> p (b c)")
        wrow = vflat[:, 1024:2048]
        eq = vflat[:, 2048:3072]
        rrow = vflat[:, 3456:3456 + NR]
        rtmp = eq[:, 0:RT * B].rearrange("p (j b) -> p j b", j=RT)
        pick4 = eq[:, 512:640].rearrange("p (v n b) -> p v n b", v=4, b=BT)
        pick0 = vflat[:, 3584:5632].rearrange("p (k n) -> p k n", k=2)
        turn = vflat[:, 3840:4352].rearrange("p (k n i) -> p k n i", k=2, n=2 * NT)
        red = vflat[:, 4352:4864].rearrange("p (k n i) -> p k n i", k=2, n=2 * NT)
        ang = vflat[:, 4864:5120].rearrange("p (n i) -> p n i", n=2 * NT)
        vz, kzc = kz, vraw
        NQB = 3
        QB = early[:, 0:NQB * 1024].rearrange("p (k b g q) -> p k b g q", k=NQB, b=BT, g=2)
        masks = early[:, NQB * 1024:NQB * 1024 + B * NKEY // 2].bitcast(bf16).rearrange("p (b c) -> p b c", b=B)
        kflat = kraw[:, :, :].rearrange("p j n -> p (j n)")

        def carve(at, n):
            return kflat[:, at:at + n], at + n

        P_, at = carve(0, 3 * 2 * NKEY)
        P = P_.rearrange("p (k g c) -> p k g c", k=3, g=2)
        PT_, at = carve(at, 2 * 512)
        PT = PT_.rearrange("p (k n) -> p k n", k=2)
        V2_, at = carve(at, 4 * 256)
        V2 = V2_.rearrange("p (k n) -> p k n", k=4)
        QT_, at = carve(at, B * 2 * T)
        QT = QT_.rearrange("p (b q) -> p b q", b=B)
        woT_, at = carve(at, 2 * D)
        woT = woT_.rearrange("p (h o) -> p h o", h=2)
        x3T_, at = carve(at, 256)
        x3T = x3T_.rearrange("p (c t) -> p c t", c=2)
        xam, at = carve(at, 128)
        oT = sb("oT", [128, 2, 128])
        nmax = sb("nmax", [128, B, 2])
        rsum = sb("rsum", [128, B, 2])
        rinv = sb("rinv", [128, B, 2])

        bank = [ctx.enter_context(nc.psum_tensor(f"bank{i}", [128, 512], f32)) for i in range(8)]

        s_vec = sem("s_vec")
        s_ca = sem("s_ca")
        s_cb = sem("s_cb")
        s_x = [sem("s_x0"), sem("s_x1")]
        s_w0 = sem("s_w0")
        s_small = sem("s_small")
        s_wqkv = sem("s_wqkv")
        s_w3 = sem("s_w3")
        s_g1 = sem("s_g1")
        s_rt = sem("s_rt")
        s_wt = sem("s_wt")
        s_k = sem("s_k")
        s_v = sem("s_v")
        s_out = sem("s_out")

        v_idx1 = sem("v_idx1")
        v_pick0 = sem("v_pick0")
        v_idxt = sem("v_idxt")
        v_hot = sem("v_hot")
        v_column = sem("v_column")
        a_perm = sem("a_perm")
        v_bd = sem("v_bd")
        v_angles = sem("v_angles")
        v_mask = sem("v_mask")
        v_blk = sem("v_blk")
        v_oh = sem("v_oh")
        v_keep = sem("v_keep")
        v_x1 = sem("v_x1")
        v_x2 = sem("v_x2")
        v_zread = sem("v_zread")
        v_sums = sem("v_sums")
        a_first = [sem("a_first_k"), sem("a_first_v")]
        v_rest = [sem("v_rest_k"), sem("v_rest_v")]
        a_second = [sem("a_second_k"), sem("a_second_v")]
        v_third = [sem("v_third_k"), sem("v_third_v")]
        v_mid = sem("v_mid")
        g_mask = sem("g_mask")
        v_rope = sem("v_rope")
        v_max = sem("v_max")
        v_v2 = sem("v_v2")
        v_norm = sem("v_norm")
        v_x3 = sem("v_x3")
        v_xam = sem("v_xam")
        v_fin = sem("v_fin")
        v_chain = sem("v_chain")

        g_ones = sem("g_ones")
        v_live = sem("v_live")
        a_oh = sem("a_oh")
        p_hit = sem("p_hit")
        p_keep = sem("p_keep")
        v_kept = sem("v_kept")
        s_wo = sem("s_wo")
        g_zk = sem("g_zk")
        g_zv = sem("g_zv")
        g_qb = sem("g_qb")

        a_ot = sem("a_ot")
        a_x3t = sem("a_x3t")
        a_trig = sem("a_trig")
        a_wrow = sem("a_wrow")
        a_xt = sem("a_xt")
        a_sq = sem("a_sq")
        a_root = sem("a_root")
        a_z = sem("a_z")
        a_dist = sem("a_dist")
        a_qt = sem("a_qt")
        a_t1 = sem("a_t1")
        a_exp = sem("a_exp")
        a_pt = sem("a_pt")

        p_pick = sem("p_pick")
        p_bias = sem("p_bias")
        p_l0 = sem("p_l0")
        p_l1 = sem("p_l1")
        p_xt = sem("p_xt")
        p_idx = sem("p_idx")
        p_z = sem("p_z")
        p_qt = sem("p_qt")
        p_t1 = sem("p_t1")
        p_s = sem("p_s")
        p_v2 = sem("p_v2")
        p_pt = sem("p_pt")
        p_o = sem("p_o")
        p_y = sem("p_y")
        p_x3t = sem("p_x3t")
        p_xa = sem("p_xa")
        p_h = sem("p_h")

        PICK_BANK = [0, 1]
        L0_BANK = [3, 4]
        L1_BANK = [5, 6]
        XT_BANK = [7, 2]
        Z_BANK = [4, 5, 6]
        QT_BANK = [0, 1]
        T1_BANK = [2, 3, 7, 4, 5, 6]
        S_BANK = [0, 1, 2]
        PT_BANK = [3, 4]
        V2_BANK, O_BANK, TAIL_BANK = 5, 6, 7

        def tail_bank(n):
            return bank[TAIL_BANK if n < NT - 1 else S_BANK[1]]

        def adapter_bank(n):
            return bank[TAIL_BANK if n < NT - 1 else S_BANK[0]]

        NT1 = 2 * BLK
        KEEP_AT = 2
        HITS = {0: range(0, 8), 1: range(8, 16)}

        def whole(m, kind):
            return new[:, 2 * m:2 * m + 2, kind, :]

        def part(i, m, kind):
            return parts[:, i, 2 * m:2 * m + 2, kind, :]

        def t1_dst(k):
            return (VT if k < BLK else KT)[:, :, NSLOT * (k % BLK):NSLOT * (k % BLK) + NSLOT]

        def t1_src(k):
            return bank[T1_BANK[k % 6]][:, 0:NR].rearrange("p (b s) -> p b s", b=B)

        OH_DVE = 14

        def clear_args(dst, raw, j):
            r = RP[j]
            return (dst[0:r, j, :].rearrange("p (o g d) -> p g o d", g=G, o=BLK),
                    raw[0:r, j, :].rearrange("p (g o d) -> p g o d", g=G, o=BLK),
                    keep[0:r, j, :].unsqueeze(1).unsqueeze(3).broadcast_to([r, G, BLK, HD]))

        block = ctx.enter_context(nc.Block())

        @block.sync
        def _(sp):
            sp.dma_start(vec_i[:, :, :], index_rows.partition_broadcast(128)).then_inc(s_vec, 16)
            sp.dma_start(ca[:, :], const_a).then_inc(s_ca, 16)
            sp.dma_start(w0_sb[:, :, :], w0.rearrange("(k s) c d -> (s c) k d", k=2)).then_inc(s_w0, 16)
            sp.dma_start(fside_sb[:, :, :], fside.rearrange("s (a d) -> s a d", a=1).broadcast_to([S0, BT, HD]))\
                .then_inc(s_w0, 16)
            sp.dma_start(xs[:, 0:4, :], x_rows[:, 0:4, :]).then_inc(s_x[0], 16)
            sp.dma_start(xs[:, 4:8, :], x_rows[:, 4:8, :]).then_inc(s_x[1], 16)
            sp.dma_start(cb[:, :], const_b).then_inc(s_cb, 16)
            sp.dma_start(wqkvT[:, :, :], wqkvT_in).then_inc(s_wqkv, 16)
            sp.dma_start(nscale[:, :, :], norm_scales.partition_broadcast(128)).then_inc(s_small, 16)
            sp.dma_start(scal[:, :], scaling_rows).then_inc(s_small, 16)
            sp.dma_start(w3T[:, :, :], w3T_in).then_inc(s_w3, 16)
            sp.dma_start(abT[:, 0:256].rearrange("p (c n) -> p c n", c=2), aT_in).then_inc(s_w3, 16)
            sp.dma_start(abT[:, 256:512], bT_in).then_inc(s_w3, 16)
            sp.wait_ge(g_zk, RT)
            sp.dma_start(woT[:, :, :], woT_in).then_inc(s_wo, 16)
            for n in range(NT):
                sp.wait_ge(v_fin, n + 1)
                sp.dma_start(out_rows[:, n, :], xs[:, n, :]).then_inc(s_out, 16)
            sp.wait_ge(s_out, 16 * NT)

        @block.gpsimd
        def _(pool):
            pool.memset(eps[:, :], HD * EPS).then_inc(g_ones, 1)
            pool.memset(strip[:, :], 0.0).then_inc(g_ones, 1)
            pool.wait_ge(g_ones, 2)
            pool.memset(strip[:, BLK - 1:BLK], 1.0).then_inc(g_ones, 1)

            def gather(dst, src, idx, done):
                pool.indirect_dma_start(out=dst, out_offset=None, in_=src,
                                        in_offset=bass.IndirectOffsetOnAxis(ap=idx, axis=0)).then_inc(done, 16)

            pool.wait_ge(v_idx1, 1)
            for n in range(NT):
                gather(wg[:, n, :], w1_rows, idx1[:, n:n + 1], s_g1)
            pool.wait_ge(v_idxt, 1)
            for j in range(RT):
                gather(rblk_i[0:RP[j], j:j + 1], table_rows, ridx[0:RP[j], j:j + 1], s_rt)
            for j in range(2):
                gather(wtab_i[:, j:j + 1], table_rows, widx[:, j:j + 1], s_wt)
            pool.wait_ge(s_rt, 16 * RT)
            for j in range(RT):
                gather(kraw[0:RP[j], j, :], k_rows, rblk_i[0:RP[j], j:j + 1], s_k)
            for j in range(RT):
                gather(vraw[0:RP[j], j, :], v_rows, rblk_i[0:RP[j], j:j + 1], s_v)
            pool.wait_ge(v_keep, 1)
            for raw, dst, landed, done in ((vraw, vz, s_v, g_zv), (kraw, kzc, s_k, g_zk)):
                pool.wait_ge(landed, 16 * RT)
                if dst is kzc:
                    pool.wait_ge(g_zv, RT)
                for j in range(RT):
                    pool.tensor_tensor(*clear_args(dst, raw, j), ALU.mult).then_inc(done, 1)

            pool.wait_ge(p_t1, BLK)

            def mask(b):
                pool.wait_ge(a_dist, b + 1)
                pool.tensor_scalar(masks[:, b, :], dist[:, b % 2, :], (WIN / 2) ** 2, BIG, ALU.is_gt, ALU.mult)\
                    .then_inc(g_mask, 1)

            for b in range(BT):
                mask(b)
            for n in range(NT):
                pool.wait_ge(a_qt, n + 1)
                if n >= NQB:
                    pool.wait_ge(p_s, BT * (n - NQB + 1))
                for g in range(G):
                    src = QT[:, BT * n:BT * n + BT, :]
                    pool.tensor_tensor(QB[:, n % NQB, :, g // 2, 64 * (g % 2):64 * (g % 2) + 64], src,
                                       A_("batch_in_tile")[:, g:g + 1].unsqueeze(2).broadcast_to([128, BT, 2 * T]),
                                       ALU.mult).then_inc(g_qb, 1)
                if n < NT - 1:
                    for b in range(BT * (n + 1), BT * (n + 2)):
                        mask(b)

        @block.scalar
        def _(act):
            act.wait_ge(s_ca, 16)
            act.wait_ge(s_cb, 16)
            act.wait_ge(v_column, 1)
            for n in range(NT):
                nc.scalar.activation(perm[:, n, :], B_("iota"), ACT.Square, bias=tok[:, 2, n:n + 1], scale=-1.0)\
                    .then_inc(a_perm, 1)
            act.wait_ge(a_perm, NT)
            for n in range(0, NT, 4):
                nc.scalar.activation(perm[:, n:n + 4, :], perm[:, n:n + 4, :], ACT.Relu, bias=1.0, scale=-1.0)\
                    .then_inc(a_perm, 4)
            act.wait_ge(p_idx, 1)
            for h in range(2):
                nc.scalar.activation(wrow[:, 512 * h:512 * h + 512], bank[h][:, :], ACT.Copy).then_inc(a_wrow, 1)
            nc.scalar.activation(rrow, bank[3][:, 0:NR], ACT.Copy).then_inc(a_wrow, 1)
            for n in range(NT):
                act.wait_ge(p_xt, n + 1)
                nc.scalar.activation(xT[:, :, 128 * n:128 * n + 128],
                                     bank[XT_BANK[n % 2]][:, 0:256].rearrange("p (c t) -> p c t", c=2),
                                     ACT.Copy).then_inc(a_xt, 1)
                nc.scalar.activation(xTo[:, :, :, BT * n:BT * n + BT, :].rearrange("p c o b i -> p c o (b i)"),
                                     bank[XT_BANK[n % 2]][:, 256:512].rearrange("p (c o e) -> p c o e", c=2, o=BLK),
                                     ACT.Copy).then_inc(a_xt, 1)
            act.wait_ge(v_live, 1)
            for o in range(OH_DVE, BLK):
                nc.scalar.activation(OH[:, o, :], rrow, ACT.Square, bias=wlive16[:, o:o + 1], scale=-1.0)\
                    .then_inc(a_oh, 1)
            for o in range(OH_DVE, BLK):
                act.wait_ge(a_oh, o - OH_DVE + 1)
                nc.scalar.activation(OH[:, o, :], OH[:, o, :], ACT.Relu, bias=1.0, scale=-1.0).then_inc(a_oh, 1)
            act.wait_ge(v_angles, 1)
            nc.scalar.activation(trig[:, :, :, :], red[:, :, :, :], ACT.Sin).then_inc(a_trig, 1)

            def queries_out(n):
                act.wait_ge(p_qt, n + 1)
                src = bank[QT_BANK[n % 2]][:, 0:256].rearrange("p (h b t) -> p b h t", h=2, b=BT)
                dst = QT[:, BT * n:BT * n + BT, :].rearrange("p b (h t) -> p b h t", h=2)
                nc.scalar.activation(dst, src, ACT.Copy).then_inc(a_qt, 1)

            def root(m):
                act.wait_ge(v_sums, m + 1)
                nc.scalar.activation(ss[:, 1, 2 * m:2 * m + 2, :], ss[:, 0, 2 * m:2 * m + 2, :], ACT.Sqrt,
                                     bias=eps[:, 0:1]).then_inc(a_root, 1)

            def first_part(m, kind):
                if kind == 0:
                    act.wait_ge(v_rope, 2 * m + 2)
                else:
                    act.wait_ge(a_z, 4 * m + 4)
                nc.scalar.activation(part(0, m, kind), whole(m, kind), ACT.Copy).then_inc(a_first[kind], 1)

            def second_part(m, kind):
                act.wait_ge(v_rest[kind], m + 1)
                nc.scalar.activation(part(1, m, kind), whole(m, kind), ACT.Copy).then_inc(a_second[kind], 1)

            act.wait_ge(g_ones, 2)
            for n in range(NT):
                if n >= 4 and n % 2 == 0:
                    root(n // 2 - 2)
                act.wait_ge(p_z, n + 1)
                z = bank[Z_BANK[n % 3]]
                nc.scalar.activation(squares(n, 1), z[:, 0:384].unsqueeze(1), ACT.Square).then_inc(a_sq, 1)
                nc.scalar.activation(qr[:, n, :], z[:, 0:256], ACT.Copy).then_inc(a_z, 1)
                nc.scalar.activation(new[:, n, :, :], z[:, 256:512].rearrange("p (k q) -> p k q", k=2), ACT.Copy)\
                    .then_inc(a_z, 1)
                if n % 2 == 1:
                    first_part(n // 2, 1)
                    if n >= 3:
                        second_part(n // 2 - 1, 1)
            root(NT // 2 - 2)
            FIRST_AT, SECOND_AT = (1, 9, 16, 24), (6, 13, 20, 26)

            def distances(b):
                act.wait_ge(v_mid, 1)
                if b >= 2:
                    act.wait_ge(g_mask, b - 1)
                nc.scalar.activation(dist[:, b % 2, :], B_("distance"), ACT.Square, bias=mid[:, 3, b:b + 1])\
                    .then_inc(a_dist, 1)

            for k in range(NT1):
                if k == 8:
                    root(NT // 2 - 1)
                if k == 5:
                    second_part(NT // 2 - 1, 1)
                if k in FIRST_AT:
                    first_part(FIRST_AT.index(k), 0)
                if k in SECOND_AT:
                    second_part(SECOND_AT.index(k), 0)
                if k == BLK:
                    act.wait_ge(g_zk, RT)
                    act.wait_ge(v_sums, NT // 2)
                if k >= BLK and k % 2 == 0:
                    queries_out((k - BLK) // 2)
                act.wait_ge(p_t1, k + 1)
                nc.scalar.activation(t1_dst(k), t1_src(k), ACT.Copy).then_inc(a_t1, 1)
                if k >= BLK and k % 2 == 0:
                    distances((k - BLK) // 2)

            def pt_out(b):
                act.wait_ge(p_pt, b + 1)
                if b >= 2:
                    act.wait_ge(p_o, b - 1)
                nc.scalar.activation(PT[0:HK, b % 2, :], bank[PT_BANK[b % 2]][0:HK, :], ACT.Copy).then_inc(a_pt, 1)

            def heads_out(n):
                act.wait_ge(p_o, BT * n + BT)
                if n >= 1:
                    act.wait_ge(p_y, n)
                nc.scalar.activation(oT[:, :, :].rearrange("p h (b t) -> p b h t", b=BT),
                                     bank[O_BANK][:, 0:256].rearrange("p (b h t) -> p b h t", b=BT, h=2),
                                     ACT.Copy).then_inc(a_ot, 1)

            def x3_out(n):
                act.wait_ge(p_x3t, n + 1)
                nc.scalar.activation(x3T[:, :, :], tail_bank(n)[:, 0:256].rearrange("p (c t) -> p c t", c=2),
                                     ACT.Copy).then_inc(a_x3t, 1)

            for i in range(B + 6):
                if i < B:
                    act.wait_ge(v_max, 2 * i + 2)
                    for g in range(2):
                        nc.scalar.activation(P[:, i % 3, g, :], P[:, i % 3, g, :],
                                             ACT.Exp, bias=nmax[:, i, g:g + 1], scale=-1.0,
                                             accum_out=rsum[:, i, g:g + 1]).then_inc(a_exp, 1)
                if 2 <= i < B + 2:
                    pt_out(i - 2)
                if i + NT < B:
                    distances(i + NT)
                if i >= 6 and (i - 6) % BT == 0:
                    heads_out((i - 6) // BT)
                if i >= 8 and (i - 8) % BT == 0:
                    x3_out((i - 8) // BT)

        @block.vector
        def _(dve):
            V = nc.vector
            chain = [0]

            def link(ins):
                chain[0] += 1
                ins.then_inc(v_chain, 1)
                dve.wait_ge(v_chain, chain[0])

            def blocks_of(dst, src):
                link(V.tensor_scalar(dst, src, (1.0 - BLK) / 2, 1.0 / BLK, ALU.add, ALU.mult))
                link(V.tensor_scalar(dst, dst, MAGIC, None, ALU.add))
                link(V.tensor_scalar(dst, dst, MAGIC, None, ALU.subtract))

            dve.wait_ge(s_vec, 16)
            dve.wait_ge(s_ca, 16)
            link(V.tensor_copy(vec[:, :, :], vec_i[:, :, :]))
            link(V.tensor_tensor(pick4[:, :, :, :], vec[:, :, :].rearrange("p v (n b) -> p v n b", b=BT),
                                 A_("batch_in_tile").unsqueeze(1).unsqueeze(1).broadcast_to([128, 4, NT, BT]),
                                 ALU.mult))
            link(V.tensor_reduce(tokv[:, :, :], pick4[:, :, :, :], AX.X, ALU.add))
            link(V.tensor_scalar(idx1f[:, :], tokv[:, 1, :], 32.0, A_("channel"), ALU.mult, ALU.add))
            V.tensor_copy(idx1[:, :], idx1f[:, :]).then_inc(v_idx1, 1)
            for k in range(2):
                picked = V.tensor_scalar(subj[:, k, :], vec[:, 0, :], A_("subject")[:, k:k + 1], None, ALU.is_equal)
            link(picked)
            for h in range(2):
                b = slice(B // 2 * h, B // 2 * h + B // 2)
                V.tensor_tensor(pick0[:, :, 512 * h:512 * h + 512].rearrange("p k (b c) -> p k b c", c=32),
                                subj[:, :, b].unsqueeze(3).broadcast_to([128, 2, B // 2, 32]),
                                A_("same_channel").unsqueeze(1).unsqueeze(1).broadcast_to([128, 2, B // 2, 32]),
                                ALU.mult).then_inc(v_pick0, 1)
            V.tensor_scalar(hot[:, :], vec[0:S0, 0, :], A_("index")[0:S0, :], None, ALU.is_equal).then_inc(v_hot, 1)
            link(V.tensor_tensor(rtmp[:, :, :], A_("read_batch").rearrange("p (j b) -> p j b", j=RT),
                                 vec[:, 2, :].unsqueeze(1).broadcast_to([128, RT, B]), ALU.mult))
            link(V.tensor_reduce(rkv[:, 0, :], rtmp[:, :, :], AX.X, ALU.add))
            link(V.tensor_scalar(rkv[:, 1, :], rkv[:, 0, :], float(1 - WIN), 0.0, ALU.add, ALU.max))
            blocks_of(rkv[:, 2, :], rkv[:, 1, :])
            link(V.tensor_tensor(rkv[:, 0, :], rkv[:, 2, :], A_("slot"), ALU.add))
            V.tensor_tensor(ridx[:, :], rkv[:, 0, :], A_("read_row"), ALU.add)
            link(V.tensor_tensor(wtmp[:, :], A_("write_batch"), vec[:, 2, :], ALU.mult))
            link(V.tensor_reduce(wkv[:, 0:1], wtmp[:, :], AX.X, ALU.add))
            blocks_of(wkv[:, 2:3], wkv[:, 0:1])
            link(V.scalar_tensor_tensor(wkv[:, 1:2], wkv[:, 2:3], float(-BLK), wkv[:, 0:1], ALU.mult, ALU.add))
            link(V.tensor_tensor(wkv[:, 3:4], wkv[:, 2:3], A_("half"), ALU.add))
            link(V.tensor_tensor(wkv[:, 4:5], wkv[:, 3:4], A_("write_row"), ALU.add))
            V.tensor_copy(widx[:, 0:1], wkv[:, 4:5])
            V.tensor_scalar(widx[:, 1:2], wkv[:, 4:5], 1.0, None, ALU.add).then_inc(v_idxt, 1)

            def block_diagonal(m, h, src):
                n = slice(4 * h, 4 * h + 4)
                V.tensor_tensor(bd[:, m, n, :].rearrange("p n (b d) -> p n b d", b=BT),
                                src.unsqueeze(2).broadcast_to([128, 4, BT, 32]),
                                A_("batch_in_tile").unsqueeze(1).unsqueeze(3).broadcast_to([128, 4, BT, 32]),
                                ALU.mult).then_inc(v_bd, 1)

            def picked_weights(h):
                dve.wait_ge(p_pick, h + 1)
                block_diagonal(0, h, bank[PICK_BANK[h]][:, 0:128].rearrange("p (n d) -> p n d", n=4))

            picked_weights(0)
            link(V.tensor_scalar(tok[:, 0, :], tokv[:, 2, :], A_("channel"), None, ALU.add))
            blocks_of(tok[:, 2, :], tok[:, 0, :])
            link(V.scalar_tensor_tensor(tok[:, 1, :], tok[:, 2, :], float(-BLK), tok[:, 0, :], ALU.mult, ALU.add))
            V.tensor_scalar(tok[:, 2, :], tok[:, 1, :], 8.0, A_("code"), ALU.mult, ALU.add).then_inc(v_column, 1)
            picked_weights(1)
            dve.wait_ge(p_bias, 1)
            link(V.tensor_tensor(bias_all[:, :, :], bank[2][:, 0:B].rearrange("p (n b) -> p n b", b=BT),
                                 A_("batch_in_tile").unsqueeze(1).broadcast_to([128, NT, BT]), ALU.mult))
            link(V.tensor_reduce(bias[:, :], bias_all[:, :, :], AX.X, ALU.add))
            V.tensor_scalar(wrap[:, :], A_("offset"), wkv[:, 1:2], None, ALU.is_lt)
            V.tensor_copy(pos[:, 0:NT], tok[:, 0, :])
            link(V.tensor_scalar(wkv[:, 5:6], wkv[:, 3:4], float(BLK), None, ALU.mult))
            link(V.scalar_tensor_tensor(pos[:, NT:2 * NT], wrap[:, :], float(BLK), A_("offset"), ALU.mult, ALU.add))
            link(V.tensor_scalar(pos[:, NT:2 * NT], pos[:, NT:2 * NT], wkv[:, 5:6], None, ALU.add))

            def add_mix0(g):
                dve.wait_ge(p_l0, g + 1)
                for n in (2 * g, 2 * g + 1):
                    V.scalar_tensor_tensor(xs[:, n, :], bank[L0_BANK[g % 2]][:, 256 * (n % 2):256 * (n % 2) + 256],
                                           bias[:, n:n + 1], xs[:, n, :], ALU.add, ALU.add).then_inc(v_x1, 1)

            def add_mix1(g):
                dve.wait_ge(p_l1, g + 1)
                V.tensor_tensor(xs[:, 2 * g:2 * g + 2, :],
                                bank[L1_BANK[g % 2]][:, :].rearrange("p (n d) -> p n d", n=2),
                                xs[:, 2 * g:2 * g + 2, :], ALU.add).then_inc(v_x2, 1)

            add_mix0(0)
            dve.wait_ge(s_g1, 16 * NT)
            block_diagonal(1, 0, wg[:, 0:4, :])
            add_mix0(1)
            block_diagonal(1, 1, wg[:, 4:8, :])
            add_mix0(2)
            add_mix0(3)
            dve.wait_ge(s_wt, 32)
            dve.wait_ge(s_rt, 16 * RT)
            link(V.tensor_copy(wtab[:, 0:2], wtab_i[:, :]))
            V.tensor_copy(rblk[0:RP[0], 0:2], rblk_i[0:RP[0], 0:2])
            link(V.tensor_tensor(wtab[:, 2:3], wtab[:, 1:2], wtab[:, 0:1], ALU.subtract))
            V.tensor_copy(rblk[0:RP[2], 2:3], rblk_i[0:RP[2], 2:3]).then_inc(v_blk, 1)
            V.tensor_scalar(wblk[:, :], wrap[:, :], wtab[:, 2:3], wtab[:, 0:1], ALU.mult, ALU.add).then_inc(v_blk, 1)
            add_mix1(0)
            add_mix1(1)
            link(V.tensor_tensor(ang[:, :, :], pos[:, :].unsqueeze(2).broadcast_to([128, 2 * NT, 16]),
                                 A_("inv_freq").unsqueeze(1).broadcast_to([128, 2 * NT, 16]), ALU.mult))
            for k in range(2):
                turned = V.tensor_scalar(turn[:, k, :, :], ang[:, :, :], float(1 / (2 * np.pi)), 0.25 * k,
                                         ALU.mult, ALU.add)
            link(turned)
            link(V.tensor_scalar(turn[:, :, :, :], turn[:, :, :, :], MAGIC, None, ALU.add))
            link(V.tensor_scalar(turn[:, :, :, :], turn[:, :, :, :], MAGIC, None, ALU.subtract))
            dve.wait_ge(a_wrow, 3)
            eq3 = eq.rearrange("p (j q) -> p j q", j=8)
            for j in range(8):
                struck = V.scalar_tensor_tensor(eq3[:, j, :], wrow[:, 128 * j:128 * j + 128], wblk[:, j:j + 1],
                                                B_("later"), ALU.is_equal, ALU.mult, accum_out=dead[:, j:j + 1])
            link(struck)
            add_mix1(2)
            link(V.scalar_tensor_tensor(wlive[:, :], dead[:, :], -10000.0, wblk[:, :], ALU.mult, ALU.add))
            V.tensor_tensor(wlive16[:, :].rearrange("p (j k) -> p j k", k=2),
                            wlive[:, :].unsqueeze(2).broadcast_to([128, 8, 2]),
                            A_("other_parity").unsqueeze(1).broadcast_to([128, 8, 2]), ALU.add).then_inc(v_live, 1)
            dve.wait_ge(v_live, 1)
            for o in range(OH_DVE):
                if o == 2:
                    add_mix1(3)
                V.tensor_scalar(OH[:, o, :], rrow, wlive16[:, o:o + 1], None, ALU.is_equal).then_inc(v_oh, 1)
            for k in range(2):
                reduced = V.scalar_tensor_tensor(red[:, k, :, :], turn[:, k, :, :], -TWO_PI_HI, ang[:, :, :],
                                                 ALU.mult, ALU.add)
            link(reduced)
            link(V.scalar_tensor_tensor(red[:, :, :, :], turn[:, :, :, :], -TWO_PI_LO, red[:, :, :, :],
                                        ALU.mult, ALU.add))
            link(V.tensor_scalar(red[:, 1, :, :], red[:, 1, :, :], float(np.pi / 2), None, ALU.add))
            V.tensor_scalar(red[:, :, :, :], red[:, :, :, :], PI_SAFE, -PI_SAFE, ALU.min, ALU.max)\
                .then_inc(v_angles, 1)
            dve.wait_ge(p_hit, BLK)
            V.tensor_scalar(kept, bank[0][0:BLK, 0:NR], -1.0, 1.0, ALU.mult, ALU.add).then_inc(v_kept, 1)
            link(V.tensor_scalar(mid[:, 0, :], vec[:, 2, :], float(1 - WIN), 0.0, ALU.add, ALU.max))
            blocks_of(mid[:, 1, :], mid[:, 0, :])
            link(V.scalar_tensor_tensor(mid[:, 2, :], mid[:, 1, :], float(BLK), vec[:, 2, :], ALU.mult, ALU.subtract))
            V.tensor_scalar(mid[:, 3, :], mid[:, 2, :], WIN / 2 - 0.5, None, ALU.add).then_inc(v_mid, 1)
            dve.wait_ge(p_keep, 1)
            V.tensor_copy(keep[0:RP[0], 0:2, :], bank[1][0:RP[0], 0:2 * BLK].rearrange("p (j o) -> p j o", j=2))
            V.tensor_copy(keep[0:RP[2], 2, :], bank[1][0:RP[2], 2 * BLK:3 * BLK]).then_inc(v_keep, 1)
            dve.wait_ge(v_keep, 1)
            dve.wait_ge(s_small, 32)
            dve.wait_ge(a_trig, 1)
            for k, factor in enumerate((-SCALE, 1.0)):
                scaled = V.tensor_scalar(nscale[:, k, :], nscale[:, k, :], 1.0, factor * float(HD) ** 0.5,
                                         ALU.add, ALU.mult)
            link(scaled)
            link(V.tensor_tensor(nsign[:, :, :], nscale[:, :, :],
                                 A_("half_sign").unsqueeze(1).broadcast_to([128, 2, HD]), ALU.mult))
            for k in range(2):
                t = slice(NT * k, NT * k + NT)
                for f, (dst, sc) in enumerate(((rope_s, nsign), (rope_c, nscale))):
                    last = V.tensor_tensor(
                        dst[:, t, :].rearrange("p n (h i) -> p n h i", h=2),
                        trig[:, f, t, :].unsqueeze(2).broadcast_to([128, NT, 2, 16]),
                        sc[:, k, :].rearrange("p (h i) -> p h i", h=2).unsqueeze(1).broadcast_to([128, NT, 2, 16]),
                        ALU.mult)
            link(last)

            def sum_squares(m):
                dve.wait_ge(a_sq, 2 * m + 2)
                V.tensor_reduce(ss[:, 0, 2 * m:2 * m + 2, :], squares(2 * m, 2).rearrange("p n (h d) -> p n h d", h=12),
                                AX.X, ALU.add).then_inc(v_sums, 1)

            def rest(m, kind):
                dve.wait_ge(a_first[kind], m + 1)
                V.tensor_tensor(whole(m, kind), whole(m, kind), part(0, m, kind), ALU.subtract)\
                    .then_inc(v_rest[kind], 1)

            def third_part(m, kind):
                dve.wait_ge(a_second[kind], m + 1)
                V.tensor_tensor(part(2, m, kind), whole(m, kind), part(1, m, kind), ALU.subtract)\
                    .then_inc(v_third[kind], 1)

            sum_squares(0)
            rest(0, 1)
            for m in range(NT // 2):
                t, u = slice(2 * m, 2 * m + 2), slice(NT + 2 * m, NT + 2 * m + 2)
                dve.wait_ge(a_z, 4 * m + 4)
                if m >= 1:
                    dve.wait_ge(v_rope, 2 * m)
                zq = qr[:, t, :].rearrange("p n (h d) -> p n h d", h=H)
                zk = new[:, t, 0, :].rearrange("p n (h d) -> p n h d", h=G)
                for r, table in ((ra, rope_c), (rb, rope_s)):
                    V.tensor_tensor(r[:, :, 0:H, :], zq, table[:, t, :].unsqueeze(2).broadcast_to([128, 2, H, HD]),
                                    ALU.mult)
                    rotated = V.tensor_tensor(r[:, :, H:12, :], zk,
                                              table[:, u, :].unsqueeze(2).broadcast_to([128, 2, G, HD]), ALU.mult)
                rotated.then_inc(v_zread, 1)
                if m < NT // 2 - 1:
                    sum_squares(m + 1)
                if m < 2:
                    rest((1, 3)[m], 1)
                    third_part((0, 2)[m], 1)
                if m >= 1:
                    rest(m - 1, 0)
                dve.wait_ge(v_zread, m + 1)
                half_turn = "p n h (k i) -> p (n h) k i"
                V.tensor_tensor(ra[:, :, :, :].rearrange(half_turn, k=2), ra[:, :, :, :].rearrange(half_turn, k=2),
                                rb[:, :, :, :].rearrange(half_turn, k=2)[:, :, ::-1, :], ALU.add)
                dve.wait_ge(a_root, m + 1)
                link(V.reciprocal(ss[:, 2, t, :], ss[:, 1, t, :]))
                for n in (2 * m, 2 * m + 1):
                    rotated = V.tensor_tensor(qr[:, n, :].rearrange("p (h g d) -> p g h d", h=2, g=G),
                                              ra[:, n % 2, 0:H, :].rearrange("p (g h) d -> p g h d", h=2),
                                              ss[:, 2, n, 0:H].rearrange("p (g h) -> p g h", h=2).unsqueeze(3)
                                              .broadcast_to([128, G, 2, HD]), ALU.mult)
                rotated.then_inc(v_rope, 1)
                V.tensor_tensor(new[:, t, 0, :].rearrange("p n (h d) -> p n h d", h=G), ra[:, :, H:12, :],
                                ss[:, 2, t, H:12].unsqueeze(3).broadcast_to([128, 2, G, HD]), ALU.mult)\
                    .then_inc(v_rope, 1)
                if m == 0:
                    rest(2, 1)
                    third_part(1, 1)
                if m == 1:
                    third_part(3, 1)
                if m >= 1:
                    third_part(m - 1, 0)
            rest(NT // 2 - 1, 0)
            third_part(NT // 2 - 1, 0)
            V.tensor_scalar(amask[:, :], vec[:, 3, :], A_("adapter"), scal[:, 0:1], ALU.is_equal, ALU.mult)\
                .then_inc(v_mask, 1)

            def normalise(b):
                dve.wait_ge(a_exp, 2 * (b + 1))
                link(V.reciprocal(rinv[:, b, :], rsum[:, b, :]))
                for g in range(2):
                    V.tensor_scalar(P[:, b % 3, g, :], P[:, b % 3, g, :], rinv[:, b, g:g + 1], None, ALU.mult)\
                        .then_inc(v_norm, 1)

            def add_attention(n):
                dve.wait_ge(p_y, n + 1)
                V.tensor_tensor(xs[:, n, :], tail_bank(n)[:, 0:256], xs[:, n, :], ALU.add).then_inc(v_x3, 1)

            def pick_adapter(n):
                dve.wait_ge(p_xa, n + 1)
                V.tensor_tensor(xam[:, :].rearrange("p (b t) -> p b t", b=BT),
                                adapter_bank(n)[:, 256:384].rearrange("p (b t) -> p b t", b=BT),
                                amask[:, BT * n:BT * n + BT].unsqueeze(2).broadcast_to([128, BT, T]),
                                ALU.mult).then_inc(v_xam, 1)

            def add_last(n):
                dve.wait_ge(p_h, n + 1)
                V.tensor_tensor(xs[:, n, :], tail_bank(n)[:, 0:256], xs[:, n, :], ALU.add).then_inc(v_fin, 1)

            for i in range(B + 7):
                if i < B:
                    dve.wait_ge(p_s, i + 1)
                    dve.wait_ge(g_mask, i + 1)
                    if i >= 3:
                        dve.wait_ge(p_pt, i - 2)
                    for g in range(2):
                        V.tensor_tensor_reduce(P[:, i % 3, g, :], bank[S_BANK[i % 3]][:, NKEY * g:NKEY * g + NKEY],
                                               masks[:, i, :], 1.0, BIG, ALU.add, ALU.min,
                                               nmax[:, i, g:g + 1]).then_inc(v_max, 1)
                if 1 <= i < B + 1:
                    normalise(i - 1)
                if i < B and i % 2 == 0:
                    dve.wait_ge(p_v2, i // 2 + 1)
                    if i >= 4:
                        dve.wait_ge(p_o, i - 2)
                    V.tensor_copy(V2[0:HK, i % 4:i % 4 + 2, :],
                                  bank[V2_BANK][0:HK, :].rearrange("p (b n) -> p b n", b=2)).then_inc(v_v2, 1)
                n, r = (i - 7) // BT, (i - 7) % BT
                if n >= 0:
                    if r == 0:
                        add_attention(n)
                    if r == 2:
                        pick_adapter(n)
                    if r == 3:
                        add_last(n)

        @block.tensor
        def _(pe):
            M = nc.tensor.matmul
            X = nc.tensor.transpose

            def half(w, c, h):
                return w[:, h, 128 * c:128 * c + 128]

            pe.wait_ge(s_w0, 32)
            for h in range(2):
                pe.wait_ge(v_pick0, h + 1)
                for n in range(4):
                    for k in range(2):
                        last = M(bank[PICK_BANK[h]][:, 32 * n:32 * n + 32],
                                 pick0[:, k, 512 * h + 128 * n:512 * h + 128 * n + 128], w0_sb[:, k, :],
                                 start=(k == 0), stop=(k == 1))
                last.then_inc(p_pick, 1)
            pe.wait_ge(v_hot, 1)
            M(bank[2][:, 0:B], fside_sb[:, :, :].rearrange("s a d -> s (a d)"), hot[:, :], start=True, stop=True)\
                .then_inc(p_bias, 1)

            def spread_block_numbers():
                pe.wait_ge(s_cb, 16)
                pe.wait_ge(v_blk, 2)
                for j in range(8):
                    X(bank[j // 4][:, 128 * (j % 4):128 * (j % 4) + 128], wblk[:, j:j + 1].broadcast_to([128, 128]), ident)
                for j in range(RT):
                    last = X(bank[3][:, BR * NSLOT * j:BR * NSLOT * j + RP[j]],
                             rblk[0:RP[j], j:j + 1].broadcast_to([RP[j], 128]), ident[0:RP[j], 0:RP[j]])
                last.then_inc(p_idx, 1)

            for m, (banks, done, added) in enumerate(((L0_BANK, p_l0, v_x1), (L1_BANK, p_l1, v_x2))):
                for g in range(4):
                    pe.wait_ge(v_bd, 2 * m + g // 2 + 1)
                    if m == 0:
                        pe.wait_ge(s_x[g // 2], 16)
                        if g >= 2:
                            pe.wait_ge(v_x1, 2 * (g - 1))
                    else:
                        pe.wait_ge(v_x1, 2 * (g + 1))
                        if g >= 2:
                            pe.wait_ge(v_x2, g - 1)
                        if g == 2:
                            spread_block_numbers()
                    for n in (2 * g, 2 * g + 1):
                        last = M(bank[banks[g % 2]][:, 256 * (n % 2):256 * (n % 2) + 256], bd[:, m, n, :],
                                 xs[:, n, :], start=True, stop=True)
                    last.then_inc(done, 1)
            pe.wait_ge(a_perm, 2 * NT)
            for n in range(NT):
                pe.wait_ge(v_x2, n // 2 + 1)
                if n >= 2:
                    pe.wait_ge(a_xt, 2 * (n - 1))
                else:
                    pe.wait_ge(v_x1, NT)
                for c in range(2):
                    X(bank[XT_BANK[n % 2]][:, 128 * c:128 * c + 128], half(xs, c, n), ident)
                for c in range(2):
                    last = M(bank[XT_BANK[n % 2]][:, 256 + 128 * c:384 + 128 * c], half(xs, c, n),
                             perm[:, n, :], start=True, stop=True, is_transpose=True)
                last.then_inc(p_xt, 1)

            def queries(n):
                pe.wait_ge(v_rope, 2 * (n // 2) + 1)
                if n >= 2:
                    pe.wait_ge(a_qt, n - 1)
                for h in range(2):
                    last = X(bank[QT_BANK[n % 2]][:, 128 * h:128 * h + 128],
                             qr[:, n, 128 * h:128 * h + 128], ident)
                last.then_inc(p_qt, 1)

            pe.wait_ge(s_wqkv, 16)
            pe.wait_ge(a_xt, 2 * NT)
            for n in range(NT):
                if n in HITS:
                    pe.wait_ge(g_ones, 3)
                    for o in HITS[n]:
                        if o < OH_DVE:
                            pe.wait_ge(v_oh, o + 1)
                        else:
                            pe.wait_ge(a_oh, BLK - OH_DVE + o - OH_DVE + 1)
                        M(bank[0][0:BLK, 0:NR], strip[:, BLK - 1 - o:2 * BLK - 1 - o], OH[:, o, :],
                          start=(o == 0), stop=(o == BLK - 1), skip_group_check=True).then_inc(p_hit, 1)
                if n == KEEP_AT:
                    pe.wait_ge(v_kept, 1)
                    for j in range(RT):
                        last = X(bank[1][0:RP[j], BLK * j:BLK * j + BLK],
                                 kept[:, BR * NSLOT * j:BR * NSLOT * j + RP[j]], ident[0:BLK, 0:BLK])
                    last.then_inc(p_keep, 1)
                if n >= 3:
                    pe.wait_ge(a_z, 2 * (n - 2))
                z = bank[Z_BANK[n % 3]]
                for c in range(2):
                    M(z[:, 0:256], xT[:, c, 128 * n:128 * n + 128], wqkvT[:, c, 0:256], start=(c == 0), stop=(c == 1))
                for c in range(2):
                    last = M(z[:, 256:512], xTo[:, c, 2 * n:2 * n + 2, :, :].rearrange("p o b i -> p (o b i)"),
                             wqkvT[:, c, 256:512], start=(c == 0), stop=(c == 1))
                last.then_inc(p_z, 1)
            for k in range(NT1):
                kind, o = k // BLK, k % BLK
                clean = (vz, kzc)[kind]
                z = bank[T1_BANK[k % 6]]
                if k == 3:
                    pe.wait_ge(a_z, 2 * NT)
                if kind == 1 and o % 2 == 0:
                    queries(o // 2)
                if k == 0:
                    pe.wait_ge(g_zv, RT)
                if k == BLK:
                    pe.wait_ge(g_zk, RT)
                if k >= 6:
                    pe.wait_ge(a_t1, k - 5)
                for j in range(RT):
                    M(z[:, BR * NSLOT * j:BR * NSLOT * j + RP[j]],
                      clean[0:RP[j], j, 128 * o:128 * o + 128], ident[0:RP[j], 0:RP[j]],
                      start=(j == 0), stop=False, is_transpose=True, skip_group_check=True)
                if o % 4 == 0:
                    pe.wait_ge(v_third[1 - kind], o // 4 + 1)
                for i in range(3):
                    last = M(z[:, 0:NR], parts[:, i, o // 2, 1 - kind, :], OH[:, o, :], start=False, stop=(i == 2),
                             skip_group_check=True)
                last.then_inc(p_t1, 1)

            def scores(b):
                if b >= 3:
                    pe.wait_ge(v_max, 2 * (b - 2))
                n = b // BT
                if b % BT == 0:
                    pe.wait_ge(g_qb, G * (n + 1))
                z = bank[S_BANK[b % 3]][:, 0:2 * NKEY].rearrange("p (g c) -> p g c", g=2)
                for g in range(2):
                    last = M(z[:, g, :], QB[:, n % NQB, b % BT, g, :], KT[:, b, :], start=True, stop=True)
                last.then_inc(p_s, 1)

            def values(b):
                if b >= 2:
                    pe.wait_ge(v_v2, b // 2)
                for q in range(4):
                    last = X(bank[V2_BANK][0:HK, 128 * q:128 * q + 128],
                             VT[:, b + q // 2, HK * (q % 2):HK * (q % 2) + HK], ident)
                last.then_inc(p_v2, 1)

            def turn_probs(b):
                pe.wait_ge(v_norm, 2 * (b + 1))
                if b >= 2:
                    pe.wait_ge(a_pt, b - 1)
                for g in range(2):
                    for c in range(2):
                        q = 2 * g + c
                        last = X(bank[PT_BANK[b % 2]][0:HK, 128 * q:128 * q + 128],
                                 P[:, b % 3, g, HK * c:HK * c + HK], ident)
                last.then_inc(p_pt, 1)

            def weigh(b):
                pe.wait_ge(a_pt, b + 1)
                pe.wait_ge(v_v2, b // 2 + 1)
                if b % BT == 0 and b >= BT:
                    pe.wait_ge(a_ot, b // BT)
                for c in range(2):
                    for g in range(G):
                        last = M(bank[O_BANK][32 * g:32 * g + 32, 64 * (b % BT):64 * (b % BT) + 64],
                                 V2[0:HK, b % 4, 128 * c + 32 * g:128 * c + 32 * g + 32],
                                 PT[0:HK, b % 2, 128 * (2 * (g // 2) + c) + 64 * (g % 2):
                                    128 * (2 * (g // 2) + c) + 64 * (g % 2) + 64],
                                 start=(c == 0), stop=(c == 1))
                last.then_inc(p_o, 1)

            def project(n):
                pe.wait_ge(a_ot, n + 1)
                if 1 <= n < NT - 1:
                    pe.wait_ge(v_fin, n)
                for h in range(2):
                    last = M(tail_bank(n)[:, 0:256], oT[:, h, :], woT[:, h, :], start=(h == 0), stop=(h == 1))
                last.then_inc(p_y, 1)

            def turn_x3(n):
                pe.wait_ge(v_x3, n + 1)
                for c in range(2):
                    last = X(tail_bank(n)[:, 128 * c:128 * c + 128], half(xs, c, n), ident)
                last.then_inc(p_x3t, 1)

            def adapter_in(n):
                pe.wait_ge(a_x3t, n + 1)
                for c in range(2):
                    last = M(adapter_bank(n)[:, 256:384], abT[:, 128 * c:128 * c + 128], x3T[:, c, :],
                             start=(c == 0), stop=(c == 1))
                last.then_inc(p_xa, 1)

            def adapter_out(n):
                if n < NT - 1:
                    pe.wait_ge(v_xam, n + 1)
                for c in range(2):
                    M(tail_bank(n)[:, 0:256], x3T[:, c, :], w3T[:, c, :], start=(c == 0), stop=False)
                pe.wait_ge(v_xam, n + 1)
                M(tail_bank(n)[:, 0:256], xam[:, :], abT[:, 256:512], start=False, stop=True).then_inc(p_h, 1)

            pe.wait_ge(v_mask, 1)
            pe.wait_ge(a_t1, NT1)
            pe.wait_ge(a_qt, NT)
            pe.wait_ge(s_w3, 48)
            pe.wait_ge(s_wo, 16)
            for i in range(B + 7):
                n, r = (i - 7) // BT, (i - 7) % BT
                if i < B:
                    scores(i)
                    if i % 2 == 0:
                        values(i)
                if 2 <= i < B + 2:
                    turn_probs(i - 2)
                if 3 <= i < B + 3:
                    weigh(i - 3)
                if n >= 0:
                    (project, turn_x3, adapter_in, adapter_out)[r](n)



def kernel(**inputs):
    import numpy as _np
    import concourse.bacc as _bacc
    from concourse import mybir as _mybir
    from concourse.bass_utils import run_bass_kernel_spmd as _run

    nc = _bacc.Bacc("TRN2", target_bir_lowering=False, num_devices=1)
    arrays, args = {}, []

    def give(name, a):
        a = _np.ascontiguousarray(a)
        name = "in_" + name
        arrays[name] = a
        args.append(nc.dram_tensor(name, a.shape, _mybir.dt.from_np(a.dtype), kind="ExternalInput").ap())

    def rows(w):
        return w.T.reshape(2, 128, w.shape[0]).transpose(1, 0, 2)

    i = inputs
    give("x", i["x"])
    give("index_rows", _np.stack([i["itok_B_0_7"], i["itok_B_1_198"], i["itok_B_37_3939"], i["itok_B_0_6"]]))
    give("fside", i["fside_8xS_0"])
    give("block_table", i["itok_Bx257_0_4111"])
    give("mix0_weights", i["L0_cond_weights"])
    give("mix1_weights", i["L1_cond_weights"])
    give("wqkvT", rows(_np.concatenate([i["L2_cond_Wq"], i["L2_cond_Wk"], i["L2_cond_Wv"]], 0)))
    give("woT", i["L2_cond_Wo"].reshape(D, G, 2, HD).transpose(1, 3, 2, 0).reshape(128, 2, D))
    give("norm_scales", _np.stack([i["L2_cond_q_norm_scale"], i["L2_cond_k_norm_scale"]]))
    give("k_blocks", i["L2_cond_k_blocks"])
    give("v_blocks", i["L2_cond_v_blocks"])
    give("w3T", rows(i["L3_cond_W"]))
    give("aT", rows(i["L3_cond_A"].reshape(NA * RANK, D)))
    give("bT", i["L3_cond_Bm"].transpose(0, 2, 1).reshape(NA * RANK, D))
    give("scaling_rows", _np.repeat(i["L3_cond_scalings"], RANK)[:, None])
    for name, a in zip(("const_a", "const_b"), constants()):
        give(name, a)
    args.append(nc.dram_tensor("out_0_dram", (B, T, D), _mybir.dt.float32, kind="ExternalOutput").ap())
    build(nc, *args)
    r = _run(nc, [arrays], core_ids=[0])
    return r.results[0]["out_0_dram"]
```
